# Optimizing a Trainium2 kernel written in Bass

```python
import numpy as np
import jax
import jax.numpy as jnp

def _softmax(x, axis=-1):
    return jax.nn.softmax(x, axis=axis)
def _gelu(x):
    return jax.nn.gelu(x, approximate=True)
def _silu(x):
    return jax.nn.silu(x)
def _sigmoid(x):
    return jax.nn.sigmoid(x)
def _layernorm(x, axis=-1, eps=1e-5):
    m = jnp.mean(x, axis=axis, keepdims=True)
    v = jnp.var(x, axis=axis, keepdims=True)
    return (x - m) / jnp.sqrt(v + eps)
def _scatter_add(tgt, idx, src, axis=0):
    return tgt.at[idx].add(src)
def _segment_sum(src, seg, n):
    return jax.ops.segment_sum(src, seg, n)

kernel_name = 'mk_adj_preln_d4_adj_256_4679fd'

def setup_inputs(seed: int = 0):
    np.random.seed(seed)
    _w = jnp.asarray
    def _rec_inputs():
        import jax
        import jax.numpy as jnp
        _gk = jax.random.key(seed)
        x = -0.000929 + 1 * jax.random.normal(jax.random.fold_in(_gk, 1), (4096, 256), jnp.float32)
        _w = (1.0 + jnp.arange(4096, dtype=jnp.float32)) ** -0.5
        _w = _w / _w.mean()
        _pij = jnp.clip(0.0078125 * _w[:, None] * _w[None, :], 0.0, 1.0)
        _a = jax.random.uniform(jax.random.fold_in(_gk, 2), (4096, 4096)) < _pij
        adj = _a.astype(jnp.int32)
        return x, adj
    x, adj = _rec_inputs()
    def _L0_gnn_setup():
        import jax, jax.numpy as jnp
        import numpy as np
        N, IN_DIM, OUT_DIM, HEADS = (4096, 256, 64, 4)
        NEG_INF = -9000000000000000.0
        key = jax.random.key(seed)
        k_x, k_a, k_w, k_att, k_b = jax.random.split(key, 5)
        X = jax.random.normal(k_x, (N, IN_DIM), dtype=jnp.float32)
        A = jax.random.randint(k_a, (N, N), 0, 2, dtype=jnp.int32)
        W = jax.random.normal(k_w, (HEADS, IN_DIM, OUT_DIM), dtype=jnp.float32) * 0.05
        a = jax.random.normal(k_att, (HEADS, 2 * OUT_DIM), dtype=jnp.float32) * 0.05
        b = jnp.zeros((HEADS, OUT_DIM), dtype=jnp.float32)
        return {'X': X, 'A': A, 'W': W, 'a': a, 'b': b}
    _L0_gnn_all = _L0_gnn_setup()
    _L0_gnn_in = {k: v for k, v in _L0_gnn_all.items() if k in ('W', 'a', 'b', )}
    del _L0_gnn_all

    def _L1_gnn_setup():
        import jax, jax.numpy as jnp
        import numpy as np
        N, D_IN, D_OUT = (10000, 256, 256)
        key = jax.random.key(seed)
        k1, k2, k3, k4 = jax.random.split(key, 4)

        def xavier(k, shape, gain=1.414):
            fan_in, fan_out = (shape[0], shape[1])
            bound = gain * np.sqrt(6.0 / (fan_in + fan_out))
            return jax.random.uniform(k, shape, jnp.float32, -bound, bound)
        return {'input': jax.random.normal(k1, (N, D_IN), jnp.float32), 'adj': jax.random.randint(k2, (N, N), 0, 2, jnp.int32), 'M': N, 'W': xavier(k3, (D_IN, D_OUT)), 'b': jnp.zeros((D_OUT,), jnp.float32), 'a': xavier(k4, (D_OUT, 1))}
    _L1_gnn_all = _L1_gnn_setup()
    _L1_gnn_in = {k: v for k, v in _L1_gnn_all.items() if k in ('W', 'b', 'a', )}
    del _L1_gnn_all

    def _L2_gnn_setup():
        import jax, jax.numpy as jnp
        import numpy as np
        N = 8192
        IN_F = 256
        OUT_F = 256
        ALPHA = 0.2
        NEG_INF = -1000000000000.0
        key = jax.random.key(seed)
        k1, k2, k3, k4, k5 = jax.random.split(key, 5)
        inp = jax.random.normal(k1, (N, IN_F), dtype=jnp.float32)
        adj = jax.random.randint(k2, (N, N), 0, 2, dtype=jnp.int32)

        def xavier(k, shape, gain=1.414):
            fan_in, fan_out = (shape[0], shape[1])
            bound = gain * np.sqrt(6.0 / (fan_in + fan_out))
            return jax.random.uniform(k, shape, jnp.float32, -bound, bound)
        W = xavier(k3, (IN_F, OUT_F))
        a = xavier(k4, (2 * OUT_F, 1))
        wtrans = xavier(k5, (2 * IN_F, OUT_F))
        return {'inp': inp, 'adj': adj, 'W': W, 'a': a, 'wtrans': wtrans}
    _L2_gnn_all = _L2_gnn_setup()
    _L2_gnn_in = {k: v for k, v in _L2_gnn_all.items() if k in ('W', 'a', 'wtrans', )}
    del _L2_gnn_all

    def _L3_gnn_setup():
        import jax, jax.numpy as jnp
        import numpy as np
        NEG_INF = -1000000000.0
        key = jax.random.key(seed)
        k1, k2, k3, k4 = jax.random.split(key, 4)
        N, F_in, F_out, H = (4096, 256, 64, 4)
        x = jax.random.normal(k1, (N, F_in), dtype=jnp.float32)
        adj = jax.random.randint(k2, (N, N), 0, 2, dtype=jnp.int32)
        W = jax.random.normal(k3, (H, F_in, F_out), dtype=jnp.float32) * 0.05
        a = jax.random.normal(k4, (H, 2 * F_out, 1), dtype=jnp.float32) * 0.05
        return {'x': x, 'adj': adj, 'W': W, 'a': a}
    _L3_gnn_all = _L3_gnn_setup()
    _L3_gnn_in = {k: v for k, v in _L3_gnn_all.items() if k in ('W', 'a', )}
    del _L3_gnn_all

    return {
        "x": x,
        "adj": adj,
        "L0_gnn_W": _L0_gnn_in["W"],
        "L0_gnn_a": _L0_gnn_in["a"],
        "L0_gnn_b": _L0_gnn_in["b"],
        "L1_gnn_W": _L1_gnn_in["W"],
        "L1_gnn_b": _L1_gnn_in["b"],
        "L1_gnn_a": _L1_gnn_in["a"],
        "L2_gnn_W": _L2_gnn_in["W"],
        "L2_gnn_a": _L2_gnn_in["a"],
        "L2_gnn_wtrans": _L2_gnn_in["wtrans"],
        "L3_gnn_W": _L3_gnn_in["W"],
        "L3_gnn_a": _L3_gnn_in["a"],
    }

def reference(x, adj, L0_gnn_W, L0_gnn_a, L0_gnn_b, L1_gnn_W, L1_gnn_b, L1_gnn_a, L2_gnn_W, L2_gnn_a, L2_gnn_wtrans, L3_gnn_W, L3_gnn_a):
    import jax
    import jax.numpy as jnp
    def _L0_gnn_ref(X, A, W, a, b):
        import jax, jax.numpy as jnp
        import numpy as np
        N, IN_DIM, OUT_DIM, HEADS = (4096, 256, 64, 4)
        NEG_INF = -9000000000000000.0
        feat = jnp.einsum('nd,hdo->hno', X, W)
        a_src, a_dst = (a[:, :OUT_DIM], a[:, OUT_DIM:])
        s_src = jnp.einsum('hno,ho->hn', feat, a_src)
        s_dst = jnp.einsum('hno,ho->hn', feat, a_dst)
        scores = jax.nn.leaky_relu(s_src[:, :, None] + s_dst[:, None, :], negative_slope=0.2)
        masked = jnp.where(A[None, :, :] > 0, scores, jnp.float32(NEG_INF))
        attn = jax.nn.softmax(masked, axis=-1)
        out = jnp.einsum('hij,hjo->hio', attn, feat) + b[:, None, :]
        return jnp.transpose(out, (1, 0, 2)).reshape(N, HEADS * OUT_DIM)

    def _L1_gnn_ref(input, adj, M, W, b, a):
        import jax, jax.numpy as jnp
        import numpy as np
        N, D_IN, D_OUT = (10000, 256, 256)
        h = jnp.tanh(input @ W + b)
        inp = input @ W
        e = (h @ a)[:, 0]
        valid = jnp.sum(h, axis=1) != 0
        mask = (adj[:M] > 0) & valid[None, :]
        neg = jnp.asarray(-1e+30, h.dtype)
        scores = jnp.where(mask, e[None, :], neg)
        m = jnp.max(scores, axis=1, keepdims=True)
        w = jnp.where(mask, jnp.exp(scores - m), 0.0)
        denom = jnp.sum(w, axis=1, keepdims=True)
        att = w / jnp.maximum(denom, 1e-30)
        return att @ inp

    def _L2_gnn_ref(inp, adj, W, a, wtrans):
        import jax, jax.numpy as jnp
        import numpy as np
        N = 8192
        IN_F = 256
        OUT_F = 256
        ALPHA = 0.2
        NEG_INF = -1000000000000.0
        h = inp @ W
        Wh1 = h @ a[:OUT_F, :]
        Wh2 = h @ a[OUT_F:, :]
        e = jax.nn.leaky_relu(Wh1 + Wh2.T, ALPHA)
        mask = adj > 0
        attention = jax.nn.softmax(jnp.where(mask, e, NEG_INF), axis=1)
        negative_attention = -jax.nn.softmax(jnp.where(mask, -e, NEG_INF), axis=1)
        h_prime = attention @ inp
        h_prime_negative = negative_attention @ inp
        h_prime_double = jnp.concatenate([h_prime, h_prime_negative], axis=1)
        new_h_prime = h_prime_double @ wtrans
        return jax.nn.elu(new_h_prime)

    def _L3_gnn_ref(x, adj, W, a):
        import jax, jax.numpy as jnp
        import numpy as np
        NEG_INF = -1000000000.0
        H, F_in, F_out = W.shape
        N = x.shape[0]
        h = jnp.einsum('nf,hfo->hno', x, W)
        a1 = a[:, :F_out, 0]
        a2 = a[:, F_out:, 0]
        f1 = jnp.einsum('hno,ho->hn', h, a1)
        f2 = jnp.einsum('hno,ho->hn', h, a2)
        e = f1[:, :, None] + f2[:, None, :]
        e = jnp.where(e >= 0, e, 0.2 * e)
        mask = (adj == 0).astype(jnp.float32) * NEG_INF
        alpha = jax.nn.softmax(e + mask[None], axis=-1)
        out = jnp.einsum('hij,hjo->hio', alpha, h)
        return jnp.transpose(out, (1, 0, 2)).reshape(N, H * F_out)

    h = jnp.maximum(_layernorm(x, axis=-1), 0.0)
    x = x + _L0_gnn_ref(h, adj, L0_gnn_W, L0_gnn_a, L0_gnn_b)
    h = jnp.maximum(_layernorm(x, axis=-1), 0.0)
    x = x + _L1_gnn_ref(h, adj, 4096, L1_gnn_W, L1_gnn_b, L1_gnn_a)
    h = jnp.maximum(_layernorm(x, axis=-1), 0.0)
    x = x + _L2_gnn_ref(h, adj, L2_gnn_W, L2_gnn_a, L2_gnn_wtrans)
    h = jnp.maximum(_layernorm(x, axis=-1), 0.0)
    x = x + _L3_gnn_ref(h, adj, L3_gnn_W, L3_gnn_a)
    return x


_drawn_inputs = setup_inputs


def setup_inputs(seed=0):
    import zlib

    import numpy as np

    out = dict(_drawn_inputs(seed))
    spreads = {'L0_gnn_b': (0.0, 0.1), 'L1_gnn_b': (0.0, 0.8)}
    factors = {'L0_gnn_a': 5.0, 'L3_gnn_a': 8.0}
    for name, (base, spread) in spreads.items():
        noise = np.random.default_rng([zlib.crc32(name.encode()), seed]).standard_normal(out[name].shape)
        drawn = base * np.exp(spread * noise) if base else spread * noise
        out[name] = jnp.asarray(drawn.astype(out[name].dtype))
    for name, factor in factors.items():
        out[name] = (out[name] * factor).astype(out[name].dtype)
    return out
```

```python
import concourse.bass as bass
from concourse import mybir
from contextlib import ExitStack


f32 = mybir.dt.float32
f32r = mybir.dt.float32r
bf16 = mybir.dt.bfloat16
fp16 = mybir.dt.float16
i32 = mybir.dt.int32
ALU = mybir.AluOpType
ACT = mybir.ActivationFunctionType
AXX = mybir.AxisListType.X

P = 128
N = 4096
D = 256
H = 4
O = D // H
T = N // P
B = 512
NB = N // B
TB = B // P
CH = 8
NC = T // CH
E1 = D + 1
E2 = D + 2
EH = O + 1
QB, QZ = 3, 2
EZ = (QB + QZ) * EH
ZSCALE = 128.0
SC = D + 2 * H
EPS = 1e-5
BIG = 2.0 ** 125


def program(nc, x, adj, W0, a0, b0, W1, b1, a1, W2, a2, wtrans, W3, a3, out):
    RMAX = bass.bass_isa.ReduceOp.max
    ctx = ExitStack()
    with ctx:
        def tensors(scope):
            return lambda name, shape, dt: scope.enter_context(nc.sbuf_tensor(name, shape, dt))

        held = []

        def sem(name):
            held.append(nc.alloc_semaphore(name))
            return held[-1]

        def clear_semaphores():
            with nc.Block() as block:
                @block.gpsimd
                def _(pool):
                    nc.clear_and_free_semaphores(held)
            held.clear()

        def at(tile, i):
            return tile[(slice(None), bass.ds(i, 1)) + (slice(None),) * (len(tile.shape) - 2)].squeeze(1)

        def linker(eng, counter):
            count = [0]

            def link(ins, base=None):
                count[0] += 1
                ins.then_inc(counter, 1)
                eng.wait_ge(counter, count[0] if base is None else base + count[0])
            return link, count

        maskT = nc.dram_tensor("maskT_scratch", [NB, P, T * B], bf16, kind="Internal").ap()
        rows = nc.dram_tensor("rows_scratch", [H, N], f32, kind="Internal").ap()
        proj = nc.dram_tensor("proj_scratch", [2, P, 2 * SC], f32, kind="Internal").ap()

        sb = tensors(ctx)
        x_sb = sb("x_sb", [P, T, D], f32)
        identb = sb("identb", [P, P], bf16)
        zerob = sb("zerob", [P, P], bf16)
        mone = sb("mone", [P, TB], f32)
        sd = sb("sd", [P, T, 2 * H], f32)
        bco = sb("bco", [P, T, H], f32)
        vco = sb("vco", [P, T, H], f32)
        rr = sb("rr", [P, H, T], f32)
        meanbc = sb("meanbc", [P, H, EH], f32)
        wa2 = sb("wa2", [P, 2, 2], f32)
        colsum = sb("colsum", [P, 2, T], f32)

        acc = [ctx.enter_context(nc.psum_tensor(f"acc{i}", [P, 512], f32)) for i in range(4)]
        tp = [ctx.enter_context(nc.psum_tensor(f"tp{i}", [P, 512], f32)) for i in range(2)]
        fo = [ctx.enter_context(nc.psum_tensor(f"fo{i}", [P, 512], f32)) for i in range(2)]

        def setup():
            w_loaded = sem("w_loaded")
            x_loaded = sem("x_loaded")
            const_ready = sem("const_ready")
            setup_done = sem("setup_done")
            proj_stored = sem("proj_stored")
            with ExitStack() as scope, nc.Block() as block:
                sb = tensors(scope)
                wcat = [sb(f"wcat_s{i}", [P, 2, SC], f32) for i in range(2)]
                av = [sb(f"a_s{i}", [P, H, 2 * O], f32) for i in range(2)]
                w2s = sb("w2s", [P, 2, D], f32)
                a2s = sb("a2s", [P, 2 * D], f32)
                tmp = sb("tmp_s", [P, H, O], f32)
                ones = sb("ones_s", [P, P], f32)
                ident = sb("ident_s", [P, P], f32)

                @block.sync
                def _(sp):
                    for i, W in ((0, W0), (1, W3)):
                        for k in range(2):
                            sp.dma_start(wcat[i][:, k, 0:D].rearrange("p (h o) -> p h o", h=H),
                                         W[:, k * P:(k + 1) * P, :].rearrange("h p o -> p h o")).then_inc(w_loaded, 16)
                    sp.dma_start(w2s[:, :, :], W2.rearrange("(k p) o -> p k o", k=2)).then_inc(w_loaded, 16)
                    sp.dma_start(av[0][:, :, :], a0.partition_broadcast(P)).then_inc(w_loaded, 16)
                    sp.dma_start(av[1][:, :, :], a3.rearrange("h e z -> h (e z)").partition_broadcast(P)).then_inc(w_loaded, 16)
                    sp.dma_start(a2s[:, :], a2.rearrange("e z -> (e z)").partition_broadcast(P)).then_inc(w_loaded, 16)
                    sp.wait_ge(setup_done, 24)
                    for i in range(2):
                        sp.dma_start(proj[i], wcat[i][:, :, :].rearrange("p k c -> p (k c)")).then_inc(proj_stored, 16)
                    sp.wait_ge(proj_stored, 32)

                @block.scalar
                def _(act):
                    act.dma_start(x_sb[:, :, :], x.rearrange("(t p) d -> p t d", p=P)).then_inc(x_loaded, 16)
                    act.wait_ge(x_loaded, 16)

                @block.gpsimd
                def _(pool):
                    nc.gpsimd.memset(zerob[:, :], 0.0)
                    nc.gpsimd.memset(mone[:, :], -1.0)
                    nc.gpsimd.memset(ones[:, :], 1.0).then_inc(const_ready, 1)
                    pool.wait_ge(const_ready, 1)
                    nc.gpsimd.affine_select(out=ident[:, :], in_=ones[:, :], compare_op=ALU.is_equal, fill=0.0,
                                            base=0, pattern=[[-1, P]], channel_multiplier=1).then_inc(const_ready, 1)
                    pool.wait_ge(const_ready, 2)
                    nc.gpsimd.tensor_copy(identb[:, :], ident[:, :])

                @block.vector
                def _(dve):
                    link, _ = linker(dve, setup_done)
                    dve.wait_ge(w_loaded, 16 * 8)
                    for i in range(2):
                        for k in range(2):
                            for q in range(2):
                                link(nc.vector.tensor_tensor(tmp[:, :, :], wcat[i][:, k, 0:D].rearrange("p (h o) -> p h o", h=H),
                                                             av[i][:, :, q * O:(q + 1) * O], ALU.mult))
                                link(nc.vector.reduce_sum(wcat[i][:, k, D + H * q:D + H * (q + 1)], tmp[:, :, :], AXX))
                    tmp2 = tmp[:, :, :].rearrange("p h o -> p (h o)")
                    for k in range(2):
                        for q in range(2):
                            link(nc.vector.tensor_tensor(tmp2, w2s[:, k, :], a2s[:, q * D:(q + 1) * D], ALU.mult))
                            link(nc.vector.reduce_sum(wa2[:, k, q:q + 1], tmp2, AXX))

        def build_mask():
            adj_loaded = [sem(f"adj_loaded{s}") for s in range(2)]
            cast_done = sem("cast_done")
            turned = sem("turned")
            copied = sem("copied")
            stored = [sem(f"mask_stored{s}") for s in range(2)]
            half_free = sem("half_free")
            sp_step = sem("sp_step_mask")
            adj_t = adj.rearrange("(t p) j -> t p j", p=P)
            slots = [tp[0], tp[1], fo[0], fo[1]]
            with ExitStack() as scope, nc.Block() as block:
                sb = tensors(scope)
                adj_sb = sb("adj_sb", [P, 2, N], i32)
                adj16 = sb("adj16", [P, NC, CH * P], bf16)
                stage = sb("stage", [P, 2, T, B], bf16)

                def row_tiles(eng, body, after=None):
                    with eng.Fori(0, NB // 2) as pair:
                        for s in range(2):
                            b = pair * 2 + s
                            for it in range(TB):
                                body(b * TB + it, b, s, it)
                            if after:
                                after(b, s)

                @block.sync
                def _(sp):
                    def load(t, b, s, it):
                        sp.wait_ge(cast_done, NC * t + NC)
                        sp.sem_inc(sp_step, 1)
                        sp.dma_start(adj_sb[:, it % 2, :], adj_t[bass.ds(t, 1)].squeeze(0)).then_inc(adj_loaded[it % 2], 16)
                    row_tiles(sp, load)

                @block.scalar
                def _(act):
                    act.sem_inc(cast_done, 2 * NC)

                    def cast(t, b, s, it):
                        act.wait_ge(adj_loaded[it % 2], 8 * (b * TB + it - it % 2) + 16)
                        for c in range(NC):
                            act.wait_ge(turned, t * NC + c + 1)
                            nc.scalar.activation(adj16[:, c, :], adj_sb[:, it % 2, c * CH * P:(c + 1) * CH * P],
                                                 ACT.Relu).then_inc(cast_done, 1)
                    row_tiles(act, cast)

                @block.tensor
                def _(pe):
                    pe.sem_inc(turned, NC)

                    def turn(t, b, s, it):
                        for c in range(NC):
                            pe.wait_ge(cast_done, t * NC + c + 1 + 2 * NC)
                            pe.wait_ge(copied, t * NC + c + 1)
                            for q in range(CH):
                                last = nc.tensor.transpose(slots[c][:, :].bitcast(bf16)[:, q * P:(q + 1) * P],
                                                           adj16[:, c, q * P:(q + 1) * P], identb[:, :])
                            last.then_inc(turned, 1)
                    row_tiles(pe, turn)

                @block.vector
                def _(dve):
                    dve.sem_inc(copied, NC)

                    def copy(t, b, s, it):
                        if it == 0:
                            dve.wait_ge(half_free, b + 1)
                        for c in range(NC):
                            dve.wait_ge(turned, t * NC + c + 1 + NC)
                            nc.vector.tensor_scalar(stage[:, s, c * CH:(c + 1) * CH, it * P:(it + 1) * P],
                                                    slots[c][:, :].bitcast(bf16).rearrange("p (q i) -> p q i", q=CH),
                                                    0.0, None, ALU.is_gt).then_inc(copied, 1)
                    row_tiles(dve, copy)

                @block.gpsimd
                def _(pool):
                    pool.sem_inc(half_free, 2)
                    with pool.Fori(0, NB // 2) as pair:
                        for s in range(2):
                            b = pair * 2 + s
                            pool.wait_ge(copied, (b * TB + TB) * NC + NC)
                            pool.sem_inc(sp_step, 1)
                            pool.dma_start(maskT[bass.ds(b, 1)].squeeze(0), stage[:, s, :, :].rearrange("p t i -> p (t i)")
                                           ).then_inc(stored[s], 16)
                            pool.wait_ge(stored[s], 16 * pair + 16)
                            pool.sem_inc(half_free, 1)

        def features(l, load_w, n, keep):
            stat = sem(f"stat{l}")
            chain = sem(f"norm_chain{l}")
            w_loaded = sem(f"wr_loaded{l}")
            id_ready = sem(f"id_ready{l}")
            var_ready = sem(f"var_ready{l}")
            rstd_ready = sem(f"rstd_ready{l}")
            norm_ready = sem(f"norm_ready{l}")
            h_ready = sem(f"h_ready{l}")
            tr_done = sem(f"tr_done{l}")
            ht_ready = sem(f"ht_ready{l}")
            feat_done = sem(f"feat_done{l}")
            fo_free = sem(f"fo_free{l}")
            th_in = sem(f"th_in{l}")
            th_ready = sem(f"th_ready{l}")
            th_used = sem(f"th_used{l}")
            dots_used = sem(f"dots_used{l}")
            x_biased = sem(f"x_biased{l}")
            with ExitStack() as scope, nc.Block() as block:
                sb = tensors(scope)
                wr = sb(f"wr{l}", [P, 2, n], f32) if l != 2 else wa2
                ident = sb(f"ident{l}", [P, P], f32)
                mhalf = sb(f"mhalf{l}", [P, T], f32)
                hbuf = sb(f"hbuf{l}", [P, 2, D], f32)
                hT = sb(f"hT{l}", [P, 2, 2, P], f32)
                st6 = sb(f"st6_{l}", [P, T, 6], f32)
                mean = sb(f"mean{l}", [P, T], f32)
                gap = sb(f"gap{l}", [P, T], f32)
                vare = sb(f"vare{l}", [P, T], f32)
                rstd = sb(f"rstd{l}", [P, T], f32)
                nmr = sb(f"nmr{l}", [P, T], f32)
                bias = sb(f"bias{l}", [P, D], f32) if l < 2 else None
                a1_bc = sb("a1_bc", [P, D], f32) if l == 1 else None
                thin = sb("thin", [P, 2, D], f32) if l == 1 else None
                th = sb("th", [P, 2, D], f32) if l == 1 else None
                dots = sb("dots", [P, 2, D], f32) if l == 1 else None
                junk = sb("dots_copy", [P, 2, D], f32) if l == 1 else None
                NW = {0: 2, 1: 3, 2: 0, 3: 1}[l]

                @block.sync
                def _(sp):
                    if NW:
                        load_w(sp, wr, bias, a1_bc, w_loaded)
                        sp.wait_ge(w_loaded, 16 * NW)

                @block.vector
                def _(dve):
                    dve.sem_inc(fo_free, 2)
                    if l == 1:
                        dve.sem_inc(th_used, 2)
                    nc.vector.tensor_copy(ident[:, :], identb[:, :]).then_inc(id_ready, 1)
                    if l == 1:
                        nc.vector.memset(keep["F"][:, :, D:E1], 1.0)
                    elif l == 2:
                        for q, value in ((0, 1.0), (1, 0.0)):
                            nc.vector.memset(keep["X"][:, :, q, D:D + 1].bitcast(f32), value)
                            nc.vector.memset(keep["X"][:, :, q, D + 1:E2].bitcast(f32), 0.0)
                    else:
                        nc.vector.memset(keep["F"][:, :, :, O:EH], 1.0)
                    with dve.Fori(0, T) as t:
                        nc.vector.bn_stats(at(st6, t), at(x_sb, t)).then_inc(stat, 1)
                    dve.wait_ge(stat, T)
                    link, _ = linker(dve, chain)
                    link(nc.vector.tensor_tensor(gap[:, :], st6[:, :, 1], st6[:, :, 4], ALU.subtract))
                    link(nc.vector.scalar_tensor_tensor(out=vare[:, :], in0=gap[:, :], scalar=0.25, in1=gap[:, :],
                                                        op0=ALU.mult, op1=ALU.mult))
                    link(nc.vector.tensor_tensor(gap[:, :], st6[:, :, 2], st6[:, :, 5], ALU.add))
                    link(nc.vector.scalar_tensor_tensor(out=vare[:, :], in0=gap[:, :], scalar=1.0 / D, in1=vare[:, :],
                                                        op0=ALU.mult, op1=ALU.add))
                    link(nc.vector.tensor_tensor(mean[:, :], st6[:, :, 1], st6[:, :, 4], ALU.add))
                    nc.vector.tensor_scalar(vare[:, :], vare[:, :], EPS, None, ALU.add).then_inc(var_ready, 1)
                    dve.wait_ge(rstd_ready, 1)
                    nc.vector.scalar_tensor_tensor(out=nmr[:, :], in0=mean[:, :], scalar=-0.5, in1=rstd[:, :],
                                                   op0=ALU.mult, op1=ALU.mult).then_inc(norm_ready, 1)
                    if NW:
                        dve.wait_ge(w_loaded, 16 * NW)
                    with dve.Fori(0, T // 2) as t0:
                        for p in range(2):
                            t = t0 * 2 + p
                            dve.wait_ge(feat_done, t + 3)
                            if l == 1:
                                dve.wait_ge(th_used, t + 1)
                                nc.vector.tensor_tensor(thin[:, p, :], fo[p][:, 0:D], bias[:, :], ALU.add).then_inc(th_in, 1)
                                nc.vector.tensor_copy(at(keep["F"], t)[:, 0:D], fo[p][:, 0:D]).then_inc(fo_free, 1)
                            elif l == 2:
                                hi = keep["X"][:, bass.ds(t, 1), 0, 0:D].squeeze(1)
                                nc.vector.tensor_copy(hi, hbuf[:, p, :]).then_inc(th_in, 1)
                                nc.vector.tensor_copy(at(sd, t)[:, 0:2], fo[p][:, 0:2])
                                dve.wait_ge(th_in, t + 1)
                                nc.vector.tensor_tensor(keep["X"][:, bass.ds(t, 1), 1, 0:D].squeeze(1), hbuf[:, p, :],
                                                        hi.bitcast(f32), ALU.subtract).then_inc(fo_free, 1)
                            else:
                                nc.vector.tensor_copy(at(keep["F"], t)[:, :, 0:O], fo[p][:, 0:D].rearrange("p (h o) -> p h o", h=H))
                                nc.vector.tensor_copy(at(sd, t), fo[p][:, D:SC]).then_inc(fo_free, 1)
                        if l == 1:
                            for p in range(2):
                                t = t0 * 2 + p
                                dve.wait_ge(th_ready, t + 1)
                                dve.wait_ge(dots_used, t + 1)
                                nc.vector.tensor_tensor(dots[:, p, :], th[:, p, :], a1_bc[:, :], ALU.mult).then_inc(th_used, 1)

                @block.gpsimd
                def _(pool):
                    nc.gpsimd.memset(mhalf[:, :], -0.5).then_inc(x_biased, 1)
                    pool.wait_ge(x_biased, 1)
                    pool.wait_ge(var_ready, 1)
                    nc.gpsimd.tensor_tensor(rstd[:, :], vare[:, :], mhalf[:, :], ALU.pow).then_inc(rstd_ready, 1)
                    if l == 0:
                        pool.wait_ge(w_loaded, 16 * NW)
                        with pool.Fori(0, T) as t:
                            pool.wait_ge(h_ready, t + 1)
                            pool.sem_inc(x_biased, 1)
                            nc.gpsimd.tensor_tensor(at(x_sb, t), at(x_sb, t), bias[:, :], ALU.add)

                @block.scalar
                def _(act):
                    act.sem_inc(ht_ready, 2)
                    if l == 1:
                        act.sem_inc(dots_used, 2)
                    act.wait_ge(norm_ready, 1)
                    with act.Fori(0, T // 2) as t0:
                        for p in range(2):
                            t = t0 * 2 + p
                            act.wait_ge(tr_done, t + 1)
                            if l == 2:
                                act.wait_ge(fo_free, t + 1)
                            nc.scalar.activation(hbuf[:, p, :], at(x_sb, t), ACT.Relu, bias=nmr[:, bass.ds(t, 1)],
                                                 scale=rstd[:, bass.ds(t, 1)]).then_inc(h_ready, 1)
                        for p in range(2):
                            t = t0 * 2 + p
                            act.wait_ge(tr_done, t + 3)
                            act.wait_ge(feat_done, t + 1)
                            for k in range(2):
                                last = nc.scalar.activation(hT[:, p, k, :], tp[p][:, k * P:(k + 1) * P], ACT.Copy,
                                                            accum_out=colsum[:, k, bass.ds(t, 1)])
                            last.then_inc(ht_ready, 1)
                        if l == 1:
                            for p in range(2):
                                t = t0 * 2 + p
                                act.wait_ge(th_in, t + 1)
                                act.wait_ge(th_used, t + 1)
                                nc.scalar.activation(th[:, p, :], thin[:, p, :], ACT.Tanh,
                                                     accum_out=keep["e"][:, 1, bass.ds(t, 1)]).then_inc(th_ready, 1)
                            for p in range(2):
                                t = t0 * 2 + p
                                act.wait_ge(th_used, t + 3)
                                nc.scalar.activation(junk[:, p, :], dots[:, p, :], ACT.Copy,
                                                     accum_out=keep["e"][:, 0, bass.ds(t, 1)]).then_inc(dots_used, 1)

                @block.tensor
                def _(pe):
                    pe.sem_inc(tr_done, 2)
                    pe.sem_inc(feat_done, 2)
                    pe.wait_ge(id_ready, 1)
                    if NW:
                        pe.wait_ge(w_loaded, 16 * NW)
                    with pe.Fori(0, T // 2) as t0:
                        for p in range(2):
                            t = t0 * 2 + p
                            pe.wait_ge(h_ready, t + 1)
                            pe.wait_ge(ht_ready, t + 1)
                            for k in range(2):
                                last = nc.tensor.transpose(tp[p][:, k * P:(k + 1) * P],
                                                           hbuf[:, p, k * P:(k + 1) * P], ident[:, :])
                            last.then_inc(tr_done, 1)
                        for p in range(2):
                            t = t0 * 2 + p
                            pe.wait_ge(ht_ready, t + 3)
                            pe.wait_ge(fo_free, t + 1)
                            for k in range(2):
                                last = nc.tensor.matmul(fo[p][:, 0:n], hT[:, p, k, :], wr[:, k, 0:n],
                                                        start=(k == 0), stop=(k == 1))
                            last.then_inc(feat_done, 1)

        def factors(l, F=None, Z=None):
            chain = sem(f"chain{l}")
            red_ready = sem(f"red_ready{l}")
            all_ready = sem(f"all_ready{l}")
            sub_ready = sem(f"sub_ready{l}")
            exp_ready = sem(f"exp_ready{l}")
            rr_ready = sem(f"rr_ready{l}")
            rt_done = sem(f"rt_done{l}")
            rT_ready = sem(f"rT_ready{l}")
            mh_ready = sem(f"mh_ready{l}")
            mean_done = sem(f"mean_done{l}")
            rows_stored = sem(f"rows_stored{l}")
            w_loaded = sem(f"wm_loaded{l}")
            bv_ready = sem(f"bv_ready{l}")
            zf_ready = sem(f"zf_ready{l}")
            zf_free = sem(f"zf_free{l}")
            first = sem(f"first{l}")
            rest_ready = sem(f"rest_ready{l}")
            second = sem(f"second{l}")
            NR = 2 * T if l == 2 else P
            n = 2 if l == 2 else H
            with ExitStack() as scope, nc.Block() as block:
                sb = tensors(scope)
                ident = sb(f"identm{l}", [P, P], f32)
                ones = sb(f"ones{l}", [P, P], f32)
                wr = sb(f"wm{l}", [P, 2, SC], f32)
                mh = sb(f"mh{l}", [P, 2], f32)
                mhb = sb(f"mhb{l}", [P, 2, P], f32)
                dsh = sb(f"dsh{l}", [P, T, H], f32)
                ssh = sb(f"ssh{l}", [P, H, T], f32)
                rT = sb(f"rT{l}", [P, P], f32)
                red = sb(f"red{l}", [P, H], f32)
                allred = sb(f"allred{l}", [P, H], f32)
                if l != 2:
                    bv = sb(f"bv{l}", [P, T, H], f32)
                    zf = sb(f"zf{l}", [P, 2, H, EH], f32)
                    bf = sb(f"bf{l}", [P, 2, H, EH], f32)
                    rest = sb(f"rest{l}", [P, 2, H, EH], f32)
                    Zh = Z[:, :, :, :].bitcast(fp16)

                @block.vector
                def _(dve):
                    link, count = linker(dve, chain)
                    nc.vector.tensor_copy(ident[:, :], identb[:, :])
                    nc.vector.memset(ones[:, :], 1.0)
                    if l == 2:
                        link(nc.vector.tensor_scalar(sd[:, :, 2:3], sd[:, :, 1:2], -1.0, None, ALU.mult))
                        nc.vector.reduce_max(red[:, 0:2], sd[:, :, 1:3].rearrange("p t h -> p h t"), AXX).then_inc(red_ready, 1)
                    else:
                        nc.vector.reduce_max(red[:, :], sd[:, :, H:2 * H].rearrange("p t h -> p h t"), AXX).then_inc(red_ready, 1)
                    link(nc.vector.reduce_sum(mh[:, :], colsum[:, :, :], AXX))
                    for k in range(2):
                        nc.vector.tensor_scalar(mhb[:, k, :], ones[:, :], mh[:, k:k + 1], 1.0 / N,
                                                ALU.mult, ALU.mult).then_inc(mh_ready, 1)
                    dve.wait_ge(all_ready, 1)
                    if l == 2:
                        nc.vector.tensor_tensor(dsh[:, :, 0:2], sd[:, :, 1:3],
                                                allred[:, 0:2].unsqueeze(1).to_broadcast([P, T, 2]), ALU.subtract).then_inc(sub_ready, 1)
                        link(nc.vector.tensor_scalar(ssh[:, 0, :], sd[:, :, 0], allred[:, 0:1], 0.0, ALU.add, ALU.max))
                        link(nc.vector.tensor_scalar(ssh[:, 1, :], sd[:, :, 0], -1.0, allred[:, 1:2], ALU.mult, ALU.add))
                        nc.vector.tensor_scalar(ssh[:, 1, :], ssh[:, 1, :], 0.0, 100.0, ALU.max, ALU.min).then_inc(sub_ready, 1)
                    else:
                        nc.vector.tensor_tensor(dsh[:, :, :], sd[:, :, H:2 * H],
                                                allred[:, :].unsqueeze(1).to_broadcast([P, T, H]), ALU.subtract).then_inc(sub_ready, 1)
                        link(nc.vector.tensor_tensor(ssh[:, :, :], sd[:, :, 0:H].rearrange("p t h -> p h t"),
                                                     allred[:, :].unsqueeze(2).to_broadcast([P, H, T]), ALU.add))
                        nc.vector.tensor_scalar(ssh[:, :, :], ssh[:, :, :], 0.0, None, ALU.max).then_inc(sub_ready, 1)
                    dve.wait_ge(rt_done, 1)
                    nc.vector.tensor_copy(rT[0:NR, :], tp[0][0:NR, 0:P]).then_inc(rT_ready, 1)
                    if l != 2:
                        dve.wait_ge(exp_ready, 1)
                        nc.vector.tensor_tensor(bv[:, :, :], bco[:, :, :], vco[:, :, :], ALU.mult).then_inc(bv_ready, 1)
                        dve.wait_ge(bv_ready, 1)
                        nc.vector.tensor_scalar(vco[:, :, :], vco[:, :, :], ZSCALE, None, ALU.mult).then_inc(bv_ready, 1)
                        nc.vector.tensor_scalar(rr[:, :, :], rr[:, :, :], 1.0 / ZSCALE, None, ALU.mult)
                        nc.vector.tensor_scalar(bco[:, :, :], bco[:, :, :], BIG, None, ALU.mult)
                    dve.wait_ge(mean_done, 1)
                    if l == 2:
                        mb = meanbc[:, :, :].rearrange("p h e -> p (h e)")
                        nc.vector.memset(mb[:, D:E1], 1.0)
                        nc.vector.tensor_copy(mb[:, 0:D], fo[0][:, 0:D])
                    else:
                        nc.vector.memset(meanbc[:, :, O:EH], 1.0)
                        nc.vector.tensor_copy(meanbc[:, :, 0:O], fo[0][:, 0:D].rearrange("p (h o) -> p h o", h=H))
                        dve.sem_inc(zf_free, 2)
                        with dve.Fori(0, T // 2) as t0:
                            for p in range(2):
                                t = t0 * 2 + p
                                dve.wait_ge(first, t * 2 + 2)
                                nc.vector.tensor_tensor(at(Zh, t)[:, :, (QB + 1) * EH:EZ], zf[:, p, :, :],
                                                        at(Zh, t)[:, :, QB * EH:(QB + 1) * EH], ALU.subtract)
                                nc.vector.tensor_tensor(rest[:, p, :, :], bf[:, p, :, :], at(Z, t)[:, :, 0:EH],
                                                        ALU.subtract).then_inc(rest_ready, 1)
                            for p in range(2):
                                t = t0 * 2 + p
                                dve.wait_ge(second, t + 1)
                                nc.vector.tensor_tensor(at(Z, t)[:, :, 2 * EH:3 * EH], rest[:, p, :, :], at(Z, t)[:, :, EH:2 * EH],
                                                        ALU.subtract).then_inc(zf_free, 1)

                @block.gpsimd
                def _(pool):
                    pool.wait_ge(red_ready, 1)
                    nc.gpsimd.partition_all_reduce(allred[:, 0:n], red[:, 0:n], P, RMAX).then_inc(all_ready, 1)
                    if l != 2:
                        pool.wait_ge(bv_ready, 2)
                        with pool.Fori(0, T // 2) as t0:
                            for p in range(2):
                                t = t0 * 2 + p
                                pool.wait_ge(zf_free, t + 1)
                                pool.sem_inc(bv_ready, 1)
                                nc.gpsimd.tensor_tensor(zf[:, p, :, :], at(F, t), at(vco, t).unsqueeze(2).to_broadcast([P, H, EH]), ALU.mult)
                                nc.gpsimd.tensor_tensor(bf[:, p, :, :], at(F, t), at(bv, t).unsqueeze(2).to_broadcast([P, H, EH]),
                                                        ALU.mult).then_inc(zf_ready, 1)

                @block.scalar
                def _(act):
                    act.wait_ge(sub_ready, 2)
                    if l == 2:
                        nc.scalar.activation(rr[:, 0:2, :], ssh[:, 0:2, :], ACT.Exp, scale=-0.8).then_inc(rr_ready, 1)
                        nc.scalar.activation(bco[:, :, 0:2], dsh[:, :, 0:2], ACT.Exp, scale=0.8)
                        nc.scalar.activation(vco[:, :, 0:2], dsh[:, :, 0:2], ACT.Exp, scale=0.2)
                    else:
                        nc.scalar.activation(rr[:, :, :], ssh[:, :, :], ACT.Exp, scale=-0.8).then_inc(rr_ready, 1)
                        nc.scalar.activation(bco[:, :, :], dsh[:, :, :], ACT.Exp, scale=0.8)
                        nc.scalar.activation(vco[:, :, :], dsh[:, :, :], ACT.Exp, scale=0.2).then_inc(exp_ready, 1)
                        with act.Fori(0, T // 2) as t0:
                            for p in range(2):
                                t = t0 * 2 + p
                                act.wait_ge(zf_ready, t + 1)
                                nc.scalar.activation(at(Zh, t)[:, :, QB * EH:(QB + 1) * EH], zf[:, p, :, :], ACT.Copy).then_inc(first, 1)
                                nc.scalar.activation(at(Z, t)[:, :, 0:EH], bf[:, p, :, :], ACT.Copy).then_inc(first, 1)
                            for p in range(2):
                                t = t0 * 2 + p
                                act.wait_ge(rest_ready, t + 1)
                                nc.scalar.activation(at(Z, t)[:, :, EH:2 * EH], rest[:, p, :, :], ACT.Copy).then_inc(second, 1)

                @block.tensor
                def _(pe):
                    pe.wait_ge(mh_ready, 2)
                    if l != 2:
                        pe.wait_ge(w_loaded, 16)
                    for k in range(2):
                        if l == 2:
                            last = nc.tensor.matmul(fo[0][:, k * P:(k + 1) * P], mhb[:, k, :], ident[:, :], start=True, stop=True)
                        else:
                            last = nc.tensor.matmul(fo[0][:, 0:D], mhb[:, k, :], wr[:, k, 0:D], start=(k == 0), stop=(k == 1))
                    last.then_inc(mean_done, 1)
                    pe.wait_ge(rr_ready, 1)
                    nc.tensor.transpose(tp[0][0:NR, 0:P], rr[:, :, :].rearrange("p h t -> p (h t)")[:, 0:NR], ident[:, :]).then_inc(rt_done, 1)

                @block.sync
                def _(sp):
                    if l != 2:
                        sp.dma_start(wr[:, :, :].rearrange("p k c -> p (k c)"), proj[0 if l == 0 else 1]).then_inc(w_loaded, 16)
                    sp.wait_ge(rT_ready, 1)
                    sp.dma_start(rows.rearrange("h (t p) -> (h t) p", p=P)[0:NR, :], rT[0:NR, :]).then_inc(rows_stored, 16)
                    sp.wait_ge(rows_stored, 16)

        def gat(l, Z):
            NS = T // 2
            R = 4
            rows_loaded = [sem(f"rows_loaded{l}_{s}") for s in range(2)]
            mask_loaded = [sem(f"mask_loaded{l}_{c}") for c in range(NC)]
            step_ready = sem(f"step_ready{l}")
            cut_ready = sem(f"cut_ready{l}")
            used = sem(f"used{l}")
            acc_ready = sem(f"acc_ready{l}")
            acc_free = sem(f"acc_free{l}")
            e_free = sem(f"e_free{l}")
            chain = sem(f"pool_chain{l}")
            sp_step = sem(f"sp_step{l}")
            flag_turn = sem(f"flag_turn{l}")
            with ExitStack() as scope, nc.Block() as block:
                sb = tensors(scope)
                mask = sb(f"mask{l}", [P, T, B], bf16)
                rbc = sb(f"rbc{l}", [P, 2, B], f32)
                cut = sb(f"cut{l}", [P, R, 2, 2, B], bf16)
                e = sb(f"e{l}", [P, TB, EZ], f32)
                su = sb(f"su{l}", [P, TB, EH], f32)
                sw = sb(f"sw{l}", [P, TB, EH], f32)
                fl = sb(f"fl{l}", [P, TB], f32)
                fm = sb(f"fm{l}", [P, TB, EH], f32)
                rc = sb(f"rc{l}", [P, TB], f32)
                Zh = Z[:, :, :, :].bitcast(fp16)
                maskd = maskT.rearrange("b p (t i) -> b p t i", t=T)

                @block.sync
                def _(sp):
                    def hold(s_, value):
                        sp.wait_ge(s_, value)
                        sp.sem_inc(sp_step, 1)

                    def load_mask(b, c):
                        sp.dma_start(mask[:, c * CH:(c + 1) * CH, :], maskd[bass.ds(b, 1), :, c * CH:(c + 1) * CH, :].squeeze(0)
                                     ).then_inc(mask_loaded[c], 16)

                    def load_rows(b, h):
                        sp.dma_start(rbc[:, h % 2, :], rows[h:h + 1, bass.ds(b * B, B)].squeeze(0).partition_broadcast(P)
                                     ).then_inc(rows_loaded[h % 2], 16)

                    load_rows(0, 0)
                    load_rows(0, 1)
                    for c in range(NC):
                        load_mask(0, c)

                    def later_rows(b):
                        for h in range(2, H):
                            hold(step_ready, (b * H + h - 1) * NS)
                            load_rows(b, h)

                    with sp.Fori(0, NB - 1) as b:
                        later_rows(b)
                        hold(step_ready, (b * H + 3) * NS)
                        load_rows(b + 1, 0)
                        for c in range(NC):
                            hold(cut_ready, 2 * ((b * H + 3) * NS + (c + 1) * R))
                            load_mask(b + 1, c)
                        hold(step_ready, (b * H + 4) * NS)
                        load_rows(b + 1, 1)
                    later_rows(NB - 1)

                @block.scalar
                def _(act):
                    act.sem_inc(acc_free, TB)

                    def step(n, h, jp, slot):
                        act.wait_ge(used, n + 1)
                        for q in range(2):
                            last = nc.scalar.activation(cut[:, slot, 0, q, :], rbc[:, h % 2, :], ACT.Sigmoid,
                                                        bias=bco[:, bass.ds(jp * 2 + q, 1), h:h + 1].squeeze(1), scale=-BIG)
                        last.then_inc(step_ready, 1)

                    with act.Fori(0, NB) as b:
                        for h in range(H):
                            u = b * H + h
                            act.wait_ge(rows_loaded[h % 2], 16 * (b * 2 + h // 2 + 1))
                            with act.Fori(0, NS // R) as it:
                                for k in range(R):
                                    step(u * NS + it * R + k, h, it * R + k, k)
                            act.wait_ge(acc_ready, u + 1)
                            act.wait_ge(e_free, u + 1)
                            for i in range(TB):
                                nc.scalar.activation(e[:, i, :], acc[i][:, 0:EZ], ACT.Copy).then_inc(acc_free, 1)

                @block.vector
                def _(dve):
                    def unit(b, h):
                        u = b * H + h

                        def run(n0, jp0):
                            for k in range(R):
                                dve.wait_ge(step_ready, n0 + k + 1)
                                m = mask[:, bass.ds((jp0 + k) * 2, 2), :]
                                nc.vector.tensor_tensor(cut[:, k, 0, :, :], cut[:, k, 0, :, :], m, ALU.mult).then_inc(cut_ready, 1)
                                dve.wait_ge(cut_ready, (n0 + k) * 2 + 1)
                                nc.vector.tensor_tensor(cut[:, k, 1, :, :], m, cut[:, k, 0, :, :], ALU.subtract).then_inc(cut_ready, 1)

                        if h == 0:
                            for c in range(NC):
                                dve.wait_ge(mask_loaded[c], 16 * (b + 1))
                                run(u * NS + c * R, c * R)
                        else:
                            with dve.Fori(0, NS // R) as it:
                                run(u * NS + it * R, it * R)

                    with dve.Fori(0, NB) as b:
                        for h in range(H):
                            unit(b, h)

                @block.tensor
                def _(pe):
                    pe.sem_inc(used, R)

                    def edge(i, start):
                        return nc.tensor.matmul(acc[i][:, 0:2], zerob[:, :], identb[:, 0:2], start=start, stop=not start,
                                                skip_group_check=True)

                    with pe.Fori(0, NB) as b:
                        for h in range(H):
                            u = b * H + h
                            for i in range(TB):
                                pe.wait_ge(acc_free, u * TB + i + 1)
                                edge(i, True)
                            with pe.Fori(0, NS // R) as it:
                                for k in range(R):
                                    n = u * NS + it * R + k
                                    for part in range(2):
                                        pe.wait_ge(cut_ready, 2 * n + part + 1)
                                        z = Zh if part else Z
                                        c0, c1 = (QB * EH, EZ) if part else (0, QB * EH)
                                        for q in range(2):
                                            for i in range(TB):
                                                last = nc.tensor.matmul(
                                                    acc[i][:, c0:c1], cut[:, k, part, q, i * P:(i + 1) * P],
                                                    z[:, bass.ds((it * R + k) * 2 + q, 1), h, c0:c1].squeeze(1),
                                                    start=False, stop=False, skip_group_check=True)
                                    last.then_inc(used, 1)
                            for i in range(TB):
                                last = edge(i, False)
                            last.then_inc(acc_ready, 1)

                @block.gpsimd
                def _(pool):
                    pool.sem_inc(e_free, 1)
                    K = 12
                    with pool.Fori(0, NB) as b:
                        for h in range(H):
                            u = b * H + h
                            link, count = linker(pool, chain)
                            base = u * K

                            def part(q):
                                return e[:, :, q * EH:(q + 1) * EH]

                            pool.wait_ge(acc_free, (u + 1) * TB + TB)
                            link(nc.gpsimd.tensor_tensor(su[:, :, :], part(1), part(2), ALU.add), base)
                            link(nc.gpsimd.tensor_tensor(sw[:, :, :], part(3), part(4), ALU.add), base)
                            link(nc.gpsimd.tensor_tensor(su[:, :, :], su[:, :, :], part(0), ALU.add), base)
                            pool.sem_inc(e_free, 1)
                            link(nc.gpsimd.tensor_tensor(sw[:, :, :], sw[:, :, :],
                                                         rr[:, h, bass.ds(b * TB, TB)].unsqueeze(2).to_broadcast([P, TB, EH]), ALU.mult), base)
                            link(nc.gpsimd.tensor_tensor(su[:, :, :], su[:, :, :], sw[:, :, :], ALU.add), base)
                            pool.sem_inc(flag_turn, 1)
                            link(nc.gpsimd.tensor_scalar(fl[:, :], su[:, :, O], 0.0, None, ALU.is_equal), base)
                            link(nc.gpsimd.tensor_tensor(fm[:, :, :], meanbc[:, h, :].unsqueeze(1).to_broadcast([P, TB, EH]),
                                                         fl[:, :].unsqueeze(2).to_broadcast([P, TB, EH]), ALU.mult), base)
                            link(nc.gpsimd.tensor_tensor(su[:, :, :], su[:, :, :], fm[:, :, :], ALU.add), base)
                            link(nc.gpsimd.tensor_tensor(rc[:, :], su[:, :, O], mone[:, :], ALU.pow), base)
                            link(nc.gpsimd.tensor_tensor(su[:, :, 0:O], su[:, :, 0:O],
                                                         rc[:, :].unsqueeze(2).to_broadcast([P, TB, O]), ALU.mult), base)
                            xs = x_sb[:, bass.ds(b * TB, TB), h * O:(h + 1) * O]
                            link(nc.gpsimd.tensor_tensor(xs, xs, su[:, :, 0:O], ALU.add), base)
                            pool.sem_inc(chain, 1)

        def weighted_features(F, e, Z1):
            red_ready = sem("red_ready1")
            all_ready = sem("all_ready1")
            sub_ready = sem("sub_ready1")
            exp_ready = sem("exp_ready1")
            w_ready = sem("w_ready1")
            zf_ready = sem("zf_ready1")
            first = sem("first1")
            rest_ready = sem("rest_ready1")
            second = sem("second1")
            zf_free = sem("zf_free1")
            with ExitStack() as scope, nc.Block() as block:
                sb = tensors(scope)
                red = sb("red1", [P, 1], f32)
                allred = sb("allred1", [P, 1], f32)
                w = sb("w1", [P, T], f32)
                zf = sb("zf1", [P, 2, E1], f32)

                @block.vector
                def _(dve):
                    nc.vector.reduce_max(red[:, :], e[:, 0, :], AXX).then_inc(red_ready, 1)
                    dve.wait_ge(all_ready, 1)
                    nc.vector.tensor_scalar(w[:, :], e[:, 0, :], allred[:, :], None, ALU.subtract).then_inc(sub_ready, 1)
                    dve.wait_ge(exp_ready, 1)
                    nc.vector.scalar_tensor_tensor(out=w[:, :], in0=e[:, 1, :], scalar=0.0, in1=w[:, :],
                                                   op0=ALU.not_equal, op1=ALU.mult).then_inc(w_ready, 1)
                    dve.sem_inc(zf_free, 2)
                    with dve.Fori(0, T // 2) as t0:
                        for p in range(2):
                            t = t0 * 2 + p
                            dve.wait_ge(first, t + 1)
                            nc.vector.tensor_tensor(zf[:, p, :], zf[:, p, :], at(Z1, t)[:, 0, :], ALU.subtract).then_inc(rest_ready, 1)
                        for p in range(2):
                            t = t0 * 2 + p
                            dve.wait_ge(second, t + 1)
                            nc.vector.tensor_tensor(at(Z1, t)[:, 2, :], zf[:, p, :], at(Z1, t)[:, 1, :], ALU.subtract).then_inc(zf_free, 1)

                @block.gpsimd
                def _(pool):
                    pool.wait_ge(red_ready, 1)
                    nc.gpsimd.partition_all_reduce(allred[:, :], red[:, :], P, RMAX).then_inc(all_ready, 1)

                @block.scalar
                def _(act):
                    act.wait_ge(sub_ready, 1)
                    nc.scalar.activation(w[:, :], w[:, :], ACT.Exp).then_inc(exp_ready, 1)
                    act.wait_ge(w_ready, 1)
                    with act.Fori(0, T // 2) as t0:
                        for p in range(2):
                            t = t0 * 2 + p
                            act.wait_ge(zf_free, t + 1)
                            nc.scalar.activation(zf[:, p, :], at(F, t), ACT.Copy, scale=w[:, bass.ds(t, 1)]).then_inc(zf_ready, 1)
                        for p in range(2):
                            t = t0 * 2 + p
                            act.wait_ge(zf_ready, t + 1)
                            nc.scalar.activation(at(Z1, t)[:, 0, :], zf[:, p, :], ACT.Copy).then_inc(first, 1)
                        for p in range(2):
                            t = t0 * 2 + p
                            act.wait_ge(rest_ready, t + 1)
                            nc.scalar.activation(at(Z1, t)[:, 1, :], zf[:, p, :], ACT.Copy).then_inc(second, 1)

        def mask_product(Z1):
            mask_loaded = [sem(f"mask_loaded1_{c}") for c in range(NC)]
            tile_used = sem("tile_used1")
            acc_ready = sem("acc_ready1")
            acc_free = sem("acc_free1")
            den_ready = sem("den_ready1")
            sp_step = sem("sp_step1")
            pe_step = sem("pe_step1")
            banks = [acc, [tp[0], tp[1], fo[0], fo[1]]]
            with ExitStack() as scope, nc.Block() as block:
                sb = tensors(scope)
                mask = sb("mask1", [P, T, B], bf16)
                den = sb("den1", [P, 2, TB], f32)
                maskd = maskT.rearrange("b p (t i) -> b p t i", t=T)

                @block.sync
                def _(sp):
                    def load_mask(b, c):
                        sp.dma_start(mask[:, c * CH:(c + 1) * CH, :], maskd[bass.ds(b, 1), :, c * CH:(c + 1) * CH, :].squeeze(0)
                                     ).then_inc(mask_loaded[c], 16)
                    for c in range(NC):
                        load_mask(0, c)
                    with sp.Fori(0, NB - 1) as b:
                        for c in range(NC):
                            sp.wait_ge(tile_used, b * T + (c + 1) * CH)
                            sp.sem_inc(sp_step, 1)
                            load_mask(b + 1, c)

                @block.tensor
                def _(pe):
                    with pe.Fori(0, NB // 2) as pair:
                        for s in range(2):
                            b = pair * 2 + s
                            pe.wait_ge(acc_free, b + 1)
                            for i in range(TB):
                                nc.tensor.matmul(banks[s][i][:, 0:2], zerob[:, :], identb[:, 0:2], start=True, stop=False,
                                                 skip_group_check=True)
                            for c in range(NC):
                                pe.wait_ge(mask_loaded[c], 16 * b + 16)
                                pe.sem_inc(pe_step, 1)
                                with pe.Fori(0, CH) as q:
                                    for i in range(TB):
                                        for part in range(3):
                                            last = nc.tensor.matmul(
                                                banks[s][i][:, 0:E1], mask[:, bass.ds(q + c * CH, 1), i * P:(i + 1) * P].squeeze(1),
                                                             Z1[:, bass.ds(q + c * CH, 1), part, :].squeeze(1),
                                                             start=False, stop=False, skip_group_check=True)
                                    last.then_inc(tile_used, 1)
                            for i in range(TB):
                                last = nc.tensor.matmul(banks[s][i][:, 0:2], zerob[:, :], identb[:, 0:2], start=False, stop=True,
                                                        skip_group_check=True)
                            last.then_inc(acc_ready, 1)

                @block.vector
                def _(dve):
                    dve.sem_inc(acc_free, 2)
                    with dve.Fori(0, NB // 2) as pair:
                        for s in range(2):
                            b = pair * 2 + s
                            dve.wait_ge(acc_ready, b + 1)
                            for i in range(TB):
                                nc.vector.tensor_scalar(den[:, s, i:i + 1], banks[s][i][:, D:E1], 1e-37, None, ALU.max).then_inc(den_ready, 1)
                            dve.wait_ge(den_ready, b * (TB + 1) + TB)
                            nc.vector.reciprocal(den[:, s, :], den[:, s, :]).then_inc(den_ready, 1)
                            dve.wait_ge(den_ready, (b + 1) * (TB + 1))
                            for i in range(TB):
                                xs = x_sb[:, bass.ds(b * TB + i, 1), :].squeeze(1)
                                last = nc.vector.scalar_tensor_tensor(out=xs, in0=banks[s][i][:, 0:D], scalar=den[:, s, i:i + 1], in1=xs,
                                                                      op0=ALU.mult, op1=ALU.add)
                            last.then_inc(acc_free, 1)

        def layer1():
            with ExitStack() as scope:
                Z1 = tensors(scope)("Z1", [P, T, 3, E1], bf16)
                with ExitStack() as inner:
                    F = tensors(inner)("F1", [P, T, E1], f32)
                    e = tensors(inner)("e1", [P, 2, T], f32)

                    def load_w(sp, wr, b_, a_, loaded):
                        sp.dma_start(wr[:, :, :], W1.rearrange("(k p) o -> p k o", k=2)).then_inc(loaded, 16)
                        sp.dma_start(b_[:, :], b1.partition_broadcast(P)).then_inc(loaded, 16)
                        sp.dma_start(a_[:, :], a1.rearrange("e z -> (e z)").partition_broadcast(P)).then_inc(loaded, 16)
                    features(1, load_w, D, {"F": F, "e": e})
                    weighted_features(F, e, Z1)
                mask_product(Z1)

        def signed_attention(X):
            R = 4
            mask_loaded = [sem(f"mask_loaded2_{c}") for c in range(NC)]
            rows_loaded = [sem(f"rows_loaded2_{s}") for s in range(2)]
            wt_loaded = sem("wt_loaded")
            wt_ready = sem("wt_ready")
            g_ready = sem("g_ready")
            hi_ready = sem("hi_ready")
            lo_ready = sem("lo_ready")
            used = sem("used2")
            acc_ready = sem("acc_ready2")
            acc_free = sem("acc_free2")
            norm_ready = sem("normalised")
            chain = sem("pool_chain2")
            flag_turn = sem("flag_turn2")
            turned = sem("turned2")
            t_ready = sem("t_ready2")
            y_ready = sem("y_ready")
            pos_ready = sem("pos_ready")
            neg_ready = sem("neg_ready")
            elu_free = sem("elu_free")
            sp_step = sem("sp_step2")
            dve_step = sem("dve_step2")
            add_step = sem("add_step")
            with ExitStack() as scope, nc.Block() as block:
                sb = tensors(scope)
                mask = sb("mask2", [P, T, B], bf16)
                rbc = sb("rbc2", [P, 2, B], f32)
                G = sb("G", [P, R, B], f32)
                Ghi = sb("Ghi", [P, R, B], f32r)
                Glo = sb("Glo", [P, R, B], f32r)
                e = sb("e2", [P, 2, TB, E1], f32)
                fl = sb("fl2", [P, TB], f32)
                fm = sb("fm2", [P, TB, E1], f32)
                rc = sb("rc2", [P, TB], f32)
                wt = sb("wt", [P, 4, D], f32)
                ident = sb("ident_2", [P, P], f32)
                eT = sb("eT", [P, 4, P], f32)
                pos = sb("pos", [P, D], f32)
                neg = sb("neg", [P, D], f32)
                maskd = maskT.rearrange("b p (t i) -> b p t i", t=T)

                @block.sync
                def _(sp):
                    def hold(s_, value):
                        sp.wait_ge(s_, value)
                        sp.sem_inc(sp_step, 1)

                    def load_mask(b, c):
                        sp.dma_start(mask[:, c * CH:(c + 1) * CH, :], maskd[bass.ds(b, 1), :, c * CH:(c + 1) * CH, :].squeeze(0)
                                     ).then_inc(mask_loaded[c], 16)

                    def load_rows(b, s):
                        sp.dma_start(rbc[:, s, :], rows[s:s + 1, bass.ds(b * B, B)].squeeze(0).partition_broadcast(P)
                                     ).then_inc(rows_loaded[s], 16)

                    sp.dma_start(wt[:, :, :], wtrans.rearrange("(k p) o -> p k o", p=P)).then_inc(wt_loaded, 16)
                    load_rows(0, 0)
                    load_rows(0, 1)
                    for c in range(NC):
                        load_mask(0, c)
                    with sp.Fori(0, NB - 1) as b:
                        hold(g_ready, (b * 2 + 1) * T)
                        load_rows(b + 1, 0)
                        for c in range(NC):
                            hold(g_ready, (b * 2 + 1) * T + (c + 1) * CH)
                            load_mask(b + 1, c)
                        load_rows(b + 1, 1)
                    sp.wait_ge(wt_loaded, 16)

                @block.vector
                def _(dve):
                    nc.vector.tensor_copy(ident[:, :], identb[:, :]).then_inc(wt_ready, 1)
                    dve.wait_ge(wt_loaded, 16)
                    nc.vector.tensor_scalar(wt[:, 2:4, :], wt[:, 2:4, :], -1.0, None, ALU.mult).then_inc(wt_ready, 1)

                    dve.sem_inc(lo_ready, R)

                    def weights(n0, s, t0, k0):
                        for p in range(2):
                            n = n0 + p
                            t = t0 + p
                            dve.wait_ge(lo_ready, n + 1)
                            nc.vector.scalar_tensor_tensor(out=G[:, k0 + p, :], in0=rbc[:, s, :], scalar=bco[:, bass.ds(t, 1), s:s + 1].squeeze(1),
                                                           in1=at(mask, t), op0=ALU.max if s == 0 else ALU.min,
                                                           op1=ALU.mult).then_inc(g_ready, 1)

                    def lows(n0, s, t0, k0):
                        for p in range(2):
                            n = n0 + p
                            t = t0 + p
                            dve.wait_ge(hi_ready, n + 1)
                            nc.vector.scalar_tensor_tensor(out=Glo[:, k0 + p, :], in0=G[:, k0 + p, :], scalar=vco[:, bass.ds(t, 1), s:s + 1].squeeze(1),
                                                           in1=Ghi[:, k0 + p, :].bitcast(f32), op0=ALU.mult,
                                                           op1=ALU.subtract).then_inc(lo_ready, 1)

                    with dve.Fori(0, NB) as b:
                        for s in range(2):
                            u = b * 2 + s
                            dve.wait_ge(rows_loaded[s], 16 * b + 16)
                            for c in range(NC):
                                if s == 0:
                                    dve.wait_ge(mask_loaded[c], 16 * b + 16)
                                dve.sem_inc(dve_step, 1)
                                with dve.Fori(0, CH // R) as it:
                                    for k in range(0, R, 2):
                                        t = it * R + c * CH + k
                                        weights(u * T + t, s, t, k)
                                        lows(u * T + t, s, t, k)

                @block.scalar
                def _(act):
                    act.sem_inc(acc_free, TB)
                    act.sem_inc(t_ready, 1)

                    def highs(u, s, t0, count):
                        with act.Fori(0, count // R) as it:
                            for k in range(R):
                                t = it * R + t0 + k
                                act.wait_ge(used, u * T + t + 1)
                                act.wait_ge(g_ready, u * T + t + 1)
                                nc.scalar.activation(Ghi[:, k, :], G[:, k, :], ACT.Copy,
                                                     scale=vco[:, bass.ds(t, 1), s:s + 1].squeeze(1)).then_inc(hi_ready, 1)

                    def take(u, s):
                        act.wait_ge(acc_ready, u + 1)
                        for i in range(TB):
                            nc.scalar.activation(e[:, s, i, :], acc[i][:, 0:E1], ACT.Copy).then_inc(acc_free, 1)

                    def elu(b):
                        for i in range(TB):
                            n = b * TB + i
                            act.wait_ge(turned, n + 1)
                            nc.scalar.activation(eT[:, :, :].rearrange("p k c -> p (k c)"), tp[i % 2][:, :], ACT.Copy).then_inc(t_ready, 1)
                            act.wait_ge(y_ready, n + 1)
                            act.wait_ge(elu_free, n + 1)
                            nc.scalar.activation(pos[:, :], fo[i % 2][:, 0:D], ACT.Relu).then_inc(pos_ready, 1)
                            nc.scalar.activation(neg[:, :], fo[i % 2][:, 0:D], ACT.Relu, scale=-1.0).then_inc(pos_ready, 1)
                            act.wait_ge(pos_ready, 2 * n + 2)
                            nc.scalar.activation(neg[:, :], neg[:, :], ACT.Exp, scale=-1.0).then_inc(neg_ready, 1)

                    highs(0, 0, 0, T)
                    take(0, 0)
                    highs(1, 1, 0, T)
                    take(1, 1)
                    with act.Fori(0, NB - 1) as b:
                        u = b * 2 + 2
                        highs(u, 0, 0, T // 2)
                        elu(b)
                        highs(u, 0, T // 2, T // 2)
                        take(u, 0)
                        highs(u + 1, 1, 0, T)
                        take(u + 1, 1)
                    elu(NB - 1)

                @block.tensor
                def _(pe):
                    pe.sem_inc(used, R)
                    pe.wait_ge(wt_ready, 2)

                    def edge(i, start):
                        return nc.tensor.matmul(acc[i][:, 0:2], zerob[:, :], identb[:, 0:2], start=start, stop=not start,
                                                skip_group_check=True)

                    def opened(u):
                        for i in range(TB):
                            pe.wait_ge(acc_free, u * TB + i + 1)
                            edge(i, True)

                    def products(u, t0, count):
                        with pe.Fori(0, count // R) as it:
                            for k in range(R):
                                t = it * R + t0 + k
                                for w, q in ((Ghi, 0), (Ghi, 1), (Glo, 0)):
                                    if w is Glo:
                                        pe.wait_ge(lo_ready, u * T + t + 1 + R)
                                    elif q == 0:
                                        pe.wait_ge(hi_ready, u * T + t + 1)
                                    for i in range(TB):
                                        last = nc.tensor.matmul(acc[i][:, 0:E2], w[:, k, i * P:(i + 1) * P],
                                                                X[:, bass.ds(t, 1), q, :].squeeze(1),
                                                                start=False, stop=False, skip_group_check=True)
                                last.then_inc(used, 1)

                    def closed():
                        for i in range(TB):
                            last = edge(i, False)
                        last.then_inc(acc_ready, 1)

                    def project(b):
                        pe.wait_ge(norm_ready, 2 * b + 2)
                        for i in range(TB):
                            n = b * TB + i
                            for s in range(2):
                                for k in range(2):
                                    last = nc.tensor.transpose(tp[i % 2][:, (s * 2 + k) * P:(s * 2 + k + 1) * P],
                                                               e[:, s, i, k * P:(k + 1) * P], ident[:, :])
                            last.then_inc(turned, 1)
                            pe.wait_ge(t_ready, n + 2)
                            for k in range(4):
                                last = nc.tensor.matmul(fo[i % 2][:, 0:D], eT[:, k, :], wt[:, k, :], start=(k == 0), stop=(k == 3))
                            last.then_inc(y_ready, 1)

                    def unit(u):
                        opened(u)
                        products(u, 0, T)
                        closed()

                    unit(0)
                    unit(1)
                    with pe.Fori(0, NB - 1) as b:
                        u = b * 2 + 2
                        opened(u)
                        products(u, 0, T // 2)
                        project(b)
                        products(u, T // 2, T // 2)
                        closed()
                        unit(u + 1)
                    project(NB - 1)

                @block.gpsimd
                def _(pool):
                    pool.sem_inc(elu_free, 1)
                    K = 5

                    def normalise(u, s):
                        link, _ = linker(pool, chain)
                        es = e[:, s, :, :]
                        pool.wait_ge(acc_free, (u + 1) * TB + TB)
                        pool.sem_inc(flag_turn, 1)
                        link(nc.gpsimd.tensor_scalar(fl[:, :], es[:, :, D], 0.0, None, ALU.is_equal), u * K)
                        link(nc.gpsimd.tensor_tensor(fm[:, :, :], meanbc[:, :, :].rearrange("p h e -> p (h e)")[:, 0:E1].unsqueeze(1)
                                                     .to_broadcast([P, TB, E1]),
                                                     fl[:, :].unsqueeze(2).to_broadcast([P, TB, E1]), ALU.mult), u * K)
                        link(nc.gpsimd.tensor_tensor(es, es, fm[:, :, :], ALU.add), u * K)
                        link(nc.gpsimd.tensor_tensor(rc[:, :], es[:, :, D], mone[:, :], ALU.pow), u * K)
                        nc.gpsimd.tensor_tensor(es[:, :, 0:D], es[:, :, 0:D], rc[:, :].unsqueeze(2).to_broadcast([P, TB, D]),
                                                ALU.mult).then_inc(norm_ready, 1)
                        pool.wait_ge(norm_ready, u + 1)
                        pool.sem_inc(chain, 1)

                    def add(b):
                        for i in range(TB):
                            n = b * TB + i
                            pool.wait_ge(neg_ready, n + 1)
                            nc.gpsimd.tensor_tensor(neg[:, :], neg[:, :], mone[:, 0:1].to_broadcast([P, D]), ALU.add).then_inc(add_step, 1)
                            pool.wait_ge(add_step, 3 * n + 1)
                            nc.gpsimd.tensor_tensor(pos[:, :], pos[:, :], neg[:, :], ALU.add).then_inc(add_step, 1)
                            pool.wait_ge(add_step, 3 * n + 2)
                            xs = x_sb[:, bass.ds(n, 1), :].squeeze(1)
                            nc.gpsimd.tensor_tensor(xs, xs, pos[:, :], ALU.add).then_inc(add_step, 1)
                            pool.wait_ge(add_step, 3 * n + 3)
                            pool.sem_inc(elu_free, 1)

                    normalise(0, 0)
                    normalise(1, 1)
                    with pool.Fori(0, NB - 1) as b:
                        add(b)
                        normalise(b * 2 + 2, 0)
                        normalise(b * 2 + 3, 1)
                    add(NB - 1)

        def layer2():
            with ExitStack() as scope:
                X = tensors(scope)("X2", [P, T, 2, E2], f32r)
                features(2, None, 2, {"X": X})
                factors(2)
                signed_attention(X)

        def store_x():
            stored = sem("stored")
            with nc.Block() as block:
                @block.sync
                def _(sp):
                    sp.dma_start(out.rearrange("(t p) d -> p t d", p=P), x_sb[:, :, :]).then_inc(stored, 16)
                    sp.wait_ge(stored, 16)

        def gat_layer(l, bias):
            with ExitStack() as scope:
                Z = tensors(scope)(f"Z{l}", [P, T, H, EZ], bf16)
                with ExitStack() as inner:
                    F = tensors(inner)(f"F{l}", [P, T, H, EH], f32)

                    def load_w(sp, wr, b_, _, loaded):
                        sp.dma_start(wr[:, :, :].rearrange("p k c -> p (k c)"), proj[0 if l == 0 else 1]).then_inc(loaded, 16)
                        if bias is not None:
                            sp.dma_start(b_[:, :], bias.rearrange("h o -> (h o)").partition_broadcast(P)).then_inc(loaded, 16)
                    features(l, load_w, SC, {"F": F})
                    factors(l, F, Z)
                gat(l, Z)

        setup()
        build_mask()
        gat_layer(0, b0)
        clear_semaphores()
        layer1()
        clear_semaphores()
        layer2()
        clear_semaphores()
        gat_layer(3, None)
        store_x()


_INS = ["x", "adj", "L0_gnn_W", "L0_gnn_a", "L0_gnn_b", "L1_gnn_W", "L1_gnn_b", "L1_gnn_a",
        "L2_gnn_W", "L2_gnn_a", "L2_gnn_wtrans", "L3_gnn_W", "L3_gnn_a"]


def kernel(**inputs):
    import numpy as _np
    import concourse.bacc as _bacc
    from concourse import mybir as _mybir
    from concourse.bass_utils import run_bass_kernel_spmd as _run

    nc = _bacc.Bacc("TRN2", target_bir_lowering=False, num_devices=1)
    arrays, args = {}, []
    for name in _INS:
        a = _np.ascontiguousarray(inputs[name])
        arrays[f"in_{name}"] = a
        args.append(nc.dram_tensor(f"in_{name}", a.shape, _mybir.dt.from_np(a.dtype), kind="ExternalInput").ap())
    args.append(nc.dram_tensor("out_x", (N, D), f32, kind="ExternalOutput").ap())
    program(nc, *args)
    r = _run(nc, [arrays], core_ids=[0])
    return r.results[0]["out_x"]
```

```python
import concourse.bass as bass
from concourse import mybir
from contextlib import ExitStack


f32 = mybir.dt.float32
f32r = mybir.dt.float32r
bf16 = mybir.dt.bfloat16
fp16 = mybir.dt.float16
i32 = mybir.dt.int32
u8 = mybir.dt.uint8
ALU = mybir.AluOpType
ACT = mybir.ActivationFunctionType
AXX = mybir.AxisListType.X

P = 128
N = 4096
D = 256
H = 4
O = D // H
T = N // P
B = 512
NB = N // B
TB = B // P
CH = 8
NC = T // CH
G = 4
E1 = D + 1
E2 = D + 2
EH = O + 1
QB, QZ = 3, 2
EZ = (QB + QZ) * EH
ZSCALE = 128.0
SC = D + 2 * H
EPS = 1e-5
BIG = 2.0 ** 125


def program(nc, x, adj, W0, a0, b0, W1, b1, a1, W2, a2, wtrans, W3, a3, out):
    RMAX = bass.bass_isa.ReduceOp.max
    ctx = ExitStack()
    with ctx:
        def tensors(scope):
            return lambda name, shape, dt: scope.enter_context(nc.sbuf_tensor(name, shape, dt))

        held = []

        def sem(name):
            held.append(nc.alloc_semaphore(name))
            return held[-1]

        def clear_semaphores():
            with nc.Block() as block:
                @block.gpsimd
                def _(pool):
                    nc.clear_and_free_semaphores(held)
            held.clear()

        def at(tile, i):
            return tile[(slice(None), bass.ds(i, 1)) + (slice(None),) * (len(tile.shape) - 2)].squeeze(1)

        def linker(eng, counter):
            count = [0]

            def link(ins, base=None):
                count[0] += 1
                ins.then_inc(counter, 1)
                eng.wait_ge(counter, count[0] if base is None else base + count[0])
            return link

        maskT = nc.dram_tensor("maskT_scratch", [NB, P, T * B], u8, kind="Internal").ap()
        rows = nc.dram_tensor("rows_scratch", [H, N], f32, kind="Internal").ap()
        proj = nc.dram_tensor("proj_scratch", [2, P, 2 * SC], f32, kind="Internal").ap()

        sb = tensors(ctx)
        x_sb = sb("x_sb", [P, T, D], f32)
        identb = sb("identb", [P, P], bf16)
        zerob = sb("zerob", [P, P], bf16)
        mone = sb("mone", [P, TB], f32)
        sd = sb("sd", [P, T, 2 * H], f32)
        bco = sb("bco", [P, T, H], f32)
        braw = sb("braw", [P, T, H], f32)
        vco = sb("vco", [P, T, H], f32)
        rr = sb("rr", [P, H, T], f32)
        meanbc = sb("meanbc", [P, H, EH], f32)
        wa2 = sb("wa2", [P, 2, 2], f32)
        colsum = sb("colsum", [P, 2, T], f32)

        acc = [ctx.enter_context(nc.psum_tensor(f"acc{i}", [P, 512], f32)) for i in range(4)]
        tp = [ctx.enter_context(nc.psum_tensor(f"tp{i}", [P, 512], f32)) for i in range(2)]
        fo = [ctx.enter_context(nc.psum_tensor(f"fo{i}", [P, 512], f32)) for i in range(2)]

        def setup():
            w_loaded = sem("w_loaded")
            x_loaded = sem("x_loaded")
            const_ready = sem("const_ready")
            setup_done = sem("setup_done")
            proj_stored = sem("proj_stored")
            with ExitStack() as scope, nc.Block() as block:
                sb = tensors(scope)
                wcat = [sb(f"wcat_s{i}", [P, 2, SC], f32) for i in range(2)]
                av = [sb(f"a_s{i}", [P, H, 2 * O], f32) for i in range(2)]
                w2s = sb("w2s", [P, 2, D], f32)
                a2s = sb("a2s", [P, 2 * D], f32)
                tmp = sb("tmp_s", [P, H, O], f32)
                ones = sb("ones_s", [P, P], f32)
                ident = sb("ident_s", [P, P], f32)

                @block.sync
                def _(sp):
                    for i, W in ((0, W0), (1, W3)):
                        for k in range(2):
                            sp.dma_start(wcat[i][:, k, 0:D].rearrange("p (h o) -> p h o", h=H),
                                         W[:, k * P:(k + 1) * P, :].rearrange("h p o -> p h o")).then_inc(w_loaded, 16)
                    sp.dma_start(w2s[:, :, :], W2.rearrange("(k p) o -> p k o", k=2)).then_inc(w_loaded, 16)
                    sp.dma_start(av[0][:, :, :], a0.partition_broadcast(P)).then_inc(w_loaded, 16)
                    sp.dma_start(av[1][:, :, :], a3.rearrange("h e z -> h (e z)").partition_broadcast(P)).then_inc(w_loaded, 16)
                    sp.dma_start(a2s[:, :], a2.rearrange("e z -> (e z)").partition_broadcast(P)).then_inc(w_loaded, 16)
                    sp.wait_ge(setup_done, 24)
                    for i in range(2):
                        sp.dma_start(proj[i], wcat[i][:, :, :].rearrange("p k c -> p (k c)")).then_inc(proj_stored, 16)
                    sp.wait_ge(proj_stored, 32)

                @block.scalar
                def _(act):
                    act.dma_start(x_sb[:, :, :], x.rearrange("(t p) d -> p t d", p=P)).then_inc(x_loaded, 16)
                    act.wait_ge(x_loaded, 16)

                @block.gpsimd
                def _(pool):
                    nc.gpsimd.memset(zerob[:, :], 0.0)
                    nc.gpsimd.memset(mone[:, :], -1.0)
                    nc.gpsimd.memset(ones[:, :], 1.0).then_inc(const_ready, 1)
                    pool.wait_ge(const_ready, 1)
                    nc.gpsimd.affine_select(out=ident[:, :], in_=ones[:, :], compare_op=ALU.is_equal, fill=0.0,
                                            base=0, pattern=[[-1, P]], channel_multiplier=1).then_inc(const_ready, 1)
                    pool.wait_ge(const_ready, 2)
                    nc.gpsimd.tensor_copy(identb[:, :], ident[:, :])

                @block.vector
                def _(dve):
                    link = linker(dve, setup_done)
                    dve.wait_ge(w_loaded, 16 * 8)
                    for i in range(2):
                        for k in range(2):
                            for q in range(2):
                                link(nc.vector.tensor_tensor(tmp[:, :, :], wcat[i][:, k, 0:D].rearrange("p (h o) -> p h o", h=H),
                                                             av[i][:, :, q * O:(q + 1) * O], ALU.mult))
                                link(nc.vector.reduce_sum(wcat[i][:, k, D + H * q:D + H * (q + 1)], tmp[:, :, :], AXX))
                    tmp2 = tmp[:, :, :].rearrange("p h o -> p (h o)")
                    for k in range(2):
                        for q in range(2):
                            link(nc.vector.tensor_tensor(tmp2, w2s[:, k, :], a2s[:, q * D:(q + 1) * D], ALU.mult))
                            link(nc.vector.reduce_sum(wa2[:, k, q:q + 1], tmp2, AXX))

        class MaskBuild:

            def __init__(self, scope, stage):
                sb = tensors(scope)
                self.stage = stage
                self.adj_sb = sb("adj_sb", [P, 2, N], i32)
                self.adj16 = sb("adj16", [P, NC, CH * P], bf16)
                self.slots = [tp[0], tp[1]]
                self.adj_loaded = [sem(f"adj_loaded{s}") for s in range(2)]
                self.cast_done = sem("cast_done")
                self.turned = sem("turned")
                self.copied = sem("copied")
                self.half_free = sem("half_free")
                self.stored = [sem(f"mask_stored{s}") for s in range(2)]
                self.sp_step = sem("sp_step_mask")

            def load(self, sp):
                adj_t = adj.rearrange("(t p) j -> t p j", p=P)
                with sp.Fori(0, T // 2) as pair:
                    for p in range(2):
                        t = pair * 2 + p
                        sp.wait_ge(self.cast_done, NC * t + NC)
                        sp.sem_inc(self.sp_step, 1)
                        sp.dma_start(self.adj_sb[:, p, :], adj_t[bass.ds(t, 1)].squeeze(0)).then_inc(self.adj_loaded[p], 16)

            def cast(self, act, b, s):
                for it in range(TB):
                    t = b * TB + it
                    act.wait_ge(self.adj_loaded[it % 2], 8 * (t - it % 2) + 16)
                    for c in range(NC):
                        act.wait_ge(self.turned, t * NC + c + 1)
                        nc.scalar.activation(self.adj16[:, c, :], self.adj_sb[:, it % 2, c * CH * P:(c + 1) * CH * P],
                                             ACT.Relu).then_inc(self.cast_done, 1)

            def turn(self, pe, b, s):
                for it in range(TB):
                    t = b * TB + it
                    for c in range(NC):
                        pe.wait_ge(self.cast_done, t * NC + c + 1 + 2 * NC)
                        pe.wait_ge(self.copied, t * NC + c + 1)
                        for q in range(CH):
                            last = nc.tensor.transpose(self.slots[c % 2][:, :].bitcast(bf16)[:, q * P:(q + 1) * P],
                                                       self.adj16[:, c, q * P:(q + 1) * P], identb[:, :])
                        last.then_inc(self.turned, 1)

            def copy(self, dve, b, s):
                for it in range(TB):
                    t = b * TB + it
                    if it == 0:
                        dve.wait_ge(self.half_free, b + 1)
                    for c in range(NC):
                        dve.wait_ge(self.turned, t * NC + c + 1 + NC)
                        nc.vector.tensor_scalar(self.stage[:, s, c * CH:(c + 1) * CH, it * P:(it + 1) * P],
                                                self.slots[c % 2][:, :].bitcast(bf16).rearrange("p (q i) -> p q i", q=CH),
                                                0.0, None, ALU.is_gt).then_inc(self.copied, 1)

            def store(self, pool, b, s):
                pool.wait_ge(self.copied, (b * TB + TB) * NC + 2)
                pool.sem_inc(self.sp_step, 1)
                pool.dma_start(maskT[bass.ds(b, 1)].squeeze(0), self.stage[:, s, :, :].rearrange("p t i -> p (t i)")
                               ).then_inc(self.stored[s], 16)
                pool.wait_ge(self.stored[s], 8 * (b - s) + 16)
                pool.sem_inc(self.half_free, 1)

        def features(l, load_w, n, keep, stage=None):
            tps = [fo[p // 2][:, p % 2 * D:(p % 2 + 1) * D] for p in range(G)]
            fos = acc
            stat = sem(f"stat{l}")
            chain = sem(f"norm_chain{l}")
            w_loaded = sem(f"wr_loaded{l}")
            id_ready = sem(f"id_ready{l}")
            var_ready = sem(f"var_ready{l}")
            rstd_ready = sem(f"rstd_ready{l}")
            norm_ready = sem(f"norm_ready{l}")
            h_ready = sem(f"h_ready{l}")
            tr_done = sem(f"tr_done{l}")
            ht_ready = sem(f"ht_ready{l}")
            feat_done = sem(f"feat_done{l}")
            fo_free = sem(f"fo_free{l}")
            th_in = sem(f"th_in{l}")
            th_ready = sem(f"th_ready{l}")
            th_used = sem(f"th_used{l}")
            dots_used = sem(f"dots_used{l}")
            x_biased = sem(f"x_biased{l}")
            held_back = 2 * G if l == 2 else G
            with ExitStack() as scope, nc.Block() as block:
                sb = tensors(scope)
                mask = MaskBuild(scope, stage) if stage is not None else None
                wr = sb(f"wr{l}", [P, 2, n], f32) if l != 2 else wa2
                ident = sb(f"ident{l}", [P, P], f32)
                mhalf = sb(f"mhalf{l}", [P, T], f32)
                hbuf = sb(f"hbuf{l}", [P, 2 * G, D], f32)
                hT = sb(f"hT{l}", [P, G, 2, P], f32)
                st6 = sb(f"st6_{l}", [P, T, 6], f32)
                mean = sb(f"mean{l}", [P, T], f32)
                gap = sb(f"gap{l}", [P, T], f32)
                vare = sb(f"vare{l}", [P, T], f32)
                rstd = sb(f"rstd{l}", [P, T], f32)
                nmr = sb(f"nmr{l}", [P, T], f32)
                bias = sb(f"bias{l}", [P, D], f32) if l < 2 else None
                a1_bc = sb("a1_bc", [P, D], f32) if l == 1 else None
                thin = sb("thin", [P, G, D], f32) if l == 1 else None
                th = sb("th", [P, G, D], f32) if l == 1 else None
                dots = sb("dots", [P, G, D], f32) if l == 1 else None
                junk = sb("dots_copy", [P, G, D], f32) if l == 1 else None
                NW = {0: 2, 1: 3, 2: 0, 3: 1}[l]

                @block.sync
                def _(sp):
                    if NW:
                        load_w(sp, wr, bias, a1_bc, w_loaded)
                        sp.wait_ge(w_loaded, 16 * NW)
                    if mask:
                        mask.load(sp)

                @block.vector
                def _(dve):
                    dve.sem_inc(fo_free, held_back)
                    if mask:
                        dve.sem_inc(mask.copied, 2)
                    if l == 1:
                        dve.sem_inc(th_used, G)
                    nc.vector.tensor_copy(ident[:, :], identb[:, :]).then_inc(id_ready, 1)
                    if l == 1:
                        nc.vector.memset(keep["F"][:, :, D:E1], 1.0)
                    elif l == 2:
                        for q, value in ((0, 1.0), (1, 0.0)):
                            nc.vector.memset(keep["X"][:, :, q, D:D + 1].bitcast(f32), value)
                            nc.vector.memset(keep["X"][:, :, q, D + 1:E2].bitcast(f32), 0.0)
                    else:
                        nc.vector.memset(keep["F"][:, :, :, O:EH], 1.0)
                    with dve.Fori(0, T // 8) as t0:
                        for p in range(8):
                            nc.vector.bn_stats(at(st6, t0 * 8 + p), at(x_sb, t0 * 8 + p)).then_inc(stat, 1)
                    dve.wait_ge(stat, T)
                    link = linker(dve, chain)
                    link(nc.vector.tensor_tensor(gap[:, :], st6[:, :, 1], st6[:, :, 4], ALU.subtract))
                    link(nc.vector.scalar_tensor_tensor(out=vare[:, :], in0=gap[:, :], scalar=0.25, in1=gap[:, :],
                                                        op0=ALU.mult, op1=ALU.mult))
                    link(nc.vector.tensor_tensor(gap[:, :], st6[:, :, 2], st6[:, :, 5], ALU.add))
                    link(nc.vector.scalar_tensor_tensor(out=vare[:, :], in0=gap[:, :], scalar=1.0 / D, in1=vare[:, :],
                                                        op0=ALU.mult, op1=ALU.add))
                    link(nc.vector.tensor_tensor(mean[:, :], st6[:, :, 1], st6[:, :, 4], ALU.add))
                    nc.vector.tensor_scalar(vare[:, :], vare[:, :], EPS, None, ALU.add).then_inc(var_ready, 1)
                    dve.wait_ge(rstd_ready, 1)
                    nc.vector.scalar_tensor_tensor(out=nmr[:, :], in0=mean[:, :], scalar=-0.5, in1=rstd[:, :],
                                                   op0=ALU.mult, op1=ALU.mult).then_inc(norm_ready, 1)
                    if NW:
                        dve.wait_ge(w_loaded, 16 * NW)
                    with dve.Fori(0, T // G // 2) as pair:
                        for s in range(2):
                            t0 = pair * 2 + s
                            if mask:
                                mask.copy(dve, t0, s)
                            for p in range(G):
                                t = t0 * G + p
                                dve.wait_ge(feat_done, t + G + 1)
                                if l == 1:
                                    dve.wait_ge(th_used, t + 1)
                                    nc.vector.tensor_tensor(thin[:, p, :], fos[p][:, 0:D], bias[:, :], ALU.add).then_inc(th_in, 1)
                                    nc.vector.tensor_copy(at(keep["F"], t)[:, 0:D], fos[p][:, 0:D]).then_inc(fo_free, 1)
                                elif l == 2:
                                    hi = keep["X"][:, bass.ds(t, 1), 0, 0:D].squeeze(1)
                                    nc.vector.tensor_copy(hi, hbuf[:, s * G + p, :]).then_inc(th_in, 1)
                                    nc.vector.tensor_copy(at(sd, t)[:, 0:2], fos[p][:, 0:2])
                                    dve.wait_ge(th_in, t + 1)
                                    nc.vector.tensor_tensor(keep["X"][:, bass.ds(t, 1), 1, 0:D].squeeze(1), hbuf[:, s * G + p, :],
                                                            hi.bitcast(f32), ALU.subtract).then_inc(fo_free, 1)
                                else:
                                    nc.vector.tensor_copy(at(keep["F"], t)[:, :, 0:O], fos[p][:, 0:D].rearrange("p (h o) -> p h o", h=H))
                                    nc.vector.tensor_copy(at(sd, t), fos[p][:, D:SC]).then_inc(fo_free, 1)
                            if l == 1:
                                for p in range(G):
                                    t = t0 * G + p
                                    dve.wait_ge(th_ready, t + 1)
                                    dve.wait_ge(dots_used, t + 1)
                                    nc.vector.tensor_tensor(dots[:, p, :], th[:, p, :], a1_bc[:, :], ALU.mult).then_inc(th_used, 1)

                @block.gpsimd
                def _(pool):
                    nc.gpsimd.memset(rstd[:, 0:1], 1.0)
                    nc.gpsimd.memset(mhalf[:, :], -0.5).then_inc(x_biased, 1)
                    pool.wait_ge(x_biased, 1)
                    nc.gpsimd.tensor_tensor(rstd[:, 0:1], rstd[:, 0:1], mhalf[:, 0:1], ALU.pow).then_inc(x_biased, 1)
                    pool.wait_ge(x_biased, 2)
                    pool.wait_ge(var_ready, 1)
                    nc.gpsimd.tensor_tensor(rstd[:, :], vare[:, :], mhalf[:, :], ALU.pow).then_inc(rstd_ready, 1)
                    if mask:
                        pool.sem_inc(mask.half_free, 2)
                        pool.wait_ge(w_loaded, 16 * NW)
                        with pool.Fori(0, T // G // 2) as pair:
                            for s in range(2):
                                t0 = pair * 2 + s
                                for p in range(G):
                                    t = t0 * G + p
                                    pool.wait_ge(h_ready, t + 1)
                                    pool.sem_inc(x_biased, 1)
                                    nc.gpsimd.tensor_tensor(at(x_sb, t), at(x_sb, t), bias[:, :], ALU.add)
                                mask.store(pool, t0, s)

                @block.scalar
                def _(act):
                    act.sem_inc(ht_ready, G)
                    if mask:
                        act.sem_inc(mask.cast_done, 2 * NC)
                    if l == 1:
                        act.sem_inc(dots_used, G)

                    def normalise(t0, s):
                        for p in range(G):
                            t = t0 * G + p
                            act.wait_ge(tr_done, t + 1)
                            if l == 2:
                                act.wait_ge(fo_free, t + 1)
                            nc.scalar.activation(hbuf[:, s * G + p, :], at(x_sb, t), ACT.Relu, bias=nmr[:, bass.ds(t, 1)],
                                                 scale=rstd[:, bass.ds(t, 1)]).then_inc(h_ready, 1)

                    def transposed(t0):
                        for p in range(G):
                            t = t0 * G + p
                            act.wait_ge(tr_done, t0 * G + (p | 1) + 2 * G + 1)
                            act.wait_ge(feat_done, t + 1)
                            for k in range(2):
                                last = nc.scalar.activation(hT[:, p, k, :], tps[p][:, k * P:(k + 1) * P], ACT.Copy,
                                                            accum_out=colsum[:, k, bass.ds(t, 1)])
                            last.then_inc(ht_ready, 1)

                    def scores(t0):
                        if l == 1:
                            for p in range(G):
                                t = t0 * G + p
                                act.wait_ge(th_in, t + 1)
                                act.wait_ge(th_used, t + 1)
                                nc.scalar.activation(th[:, p, :], thin[:, p, :], ACT.Tanh,
                                                     accum_out=keep["e"][:, 1, bass.ds(t, 1)]).then_inc(th_ready, 1)
                            for p in range(G):
                                t = t0 * G + p
                                act.wait_ge(th_used, t + G + 1)
                                nc.scalar.activation(junk[:, p, :], dots[:, p, :], ACT.Copy,
                                                     accum_out=keep["e"][:, 0, bass.ds(t, 1)]).then_inc(dots_used, 1)

                    if mask:
                        mask.cast(act, 0, 0)
                    act.wait_ge(norm_ready, 1)
                    normalise(0, 0)
                    with act.Fori(0, T // G // 2 - 1) as pair:
                        for s in range(2):
                            t0 = pair * 2 + s
                            if l == 1:
                                transposed(t0)
                                normalise(t0 + 1, 1 - s)
                                scores(t0)
                            else:
                                normalise(t0 + 1, 1 - s)
                                transposed(t0)
                            if mask:
                                mask.cast(act, t0 + 1, 1 - s)
                    normalise(T // G - 1, 1)
                    transposed(T // G - 2)
                    scores(T // G - 2)
                    if mask:
                        mask.cast(act, T // G - 1, 1)
                    transposed(T // G - 1)
                    scores(T // G - 1)

                @block.tensor
                def _(pe):
                    pe.sem_inc(tr_done, 2 * G)
                    if mask:
                        pe.sem_inc(mask.turned, NC)
                    pe.sem_inc(feat_done, G)
                    pe.wait_ge(id_ready, 1)
                    if NW:
                        pe.wait_ge(w_loaded, 16 * NW)
                    with pe.Fori(0, T // G // 2) as pair:
                        for s in range(2):
                            t0 = pair * 2 + s
                            if mask:
                                mask.turn(pe, t0, s)
                            for p in range(G):
                                t = t0 * G + p
                                pe.wait_ge(h_ready, t + 1)
                                pe.wait_ge(ht_ready, t0 * G + (p | 1) + 1)
                                for k in range(2):
                                    last = nc.tensor.transpose(tps[p][:, k * P:(k + 1) * P],
                                                               hbuf[:, s * G + p, k * P:(k + 1) * P], ident[:, :])
                                last.then_inc(tr_done, 1)
                            for p in range(G):
                                t = t0 * G + p
                                pe.wait_ge(ht_ready, t + G + 1)
                                pe.wait_ge(fo_free, t + 1 + held_back - G)
                                for k in range(2):
                                    last = nc.tensor.matmul(fos[p][:, 0:n], hT[:, p, k, :], wr[:, k, 0:n],
                                                            start=(k == 0), stop=(k == 1))
                                last.then_inc(feat_done, 1)

        def factors(l, F=None, Z=None):
            chain = sem(f"chain{l}")
            red_ready = sem(f"red_ready{l}")
            all_ready = sem(f"all_ready{l}")
            sub_ready = sem(f"sub_ready{l}")
            exp_ready = sem(f"exp_ready{l}")
            rr_ready = sem(f"rr_ready{l}")
            rt_done = sem(f"rt_done{l}")
            rT_ready = sem(f"rT_ready{l}")
            mh_ready = sem(f"mh_ready{l}")
            mean_done = sem(f"mean_done{l}")
            rows_stored = sem(f"rows_stored{l}")
            w_loaded = sem(f"wm_loaded{l}")
            bv_ready = sem(f"bv_ready{l}")
            zf_ready = sem(f"zf_ready{l}")
            zf_free = sem(f"zf_free{l}")
            first = sem(f"first{l}")
            rest_ready = sem(f"rest_ready{l}")
            second = sem(f"second{l}")
            NR = 2 * T if l == 2 else P
            n = 2 if l == 2 else H
            with ExitStack() as scope, nc.Block() as block:
                sb = tensors(scope)
                ident = sb(f"identm{l}", [P, P], f32)
                ones = sb(f"ones{l}", [P, P], f32)
                wr = sb(f"wm{l}", [P, 2, SC], f32)
                mh = sb(f"mh{l}", [P, 2], f32)
                mhb = sb(f"mhb{l}", [P, 2, P], f32)
                dsh = sb(f"dsh{l}", [P, T, H], f32)
                ssh = sb(f"ssh{l}", [P, H, T], f32)
                rT = sb(f"rT{l}", [P, P], f32)
                red = sb(f"red{l}", [P, H], f32)
                allred = sb(f"allred{l}", [P, H], f32)
                if l != 2:
                    bv = sb(f"bv{l}", [P, T, H], f32)
                    zf = sb(f"zf{l}", [P, 2 * G, H, EH], f32)
                    bf = sb(f"bf{l}", [P, 2 * G, H, EH], f32)
                    rest = sb(f"rest{l}", [P, 2 * G, H, EH], f32)
                    Zh = Z[:, :, :, :].bitcast(fp16)

                @block.vector
                def _(dve):
                    link = linker(dve, chain)
                    nc.vector.tensor_copy(ident[:, :], identb[:, :])
                    nc.vector.memset(ones[:, :], 1.0)
                    if l == 2:
                        link(nc.vector.tensor_scalar(sd[:, :, 2:3], sd[:, :, 1:2], -1.0, None, ALU.mult))
                        nc.vector.reduce_max(red[:, 0:2], sd[:, :, 1:3].rearrange("p t h -> p h t"), AXX).then_inc(red_ready, 1)
                    else:
                        nc.vector.reduce_max(red[:, :], sd[:, :, H:2 * H].rearrange("p t h -> p h t"), AXX).then_inc(red_ready, 1)
                    link(nc.vector.reduce_sum(mh[:, :], colsum[:, :, :], AXX))
                    for k in range(2):
                        nc.vector.tensor_scalar(mhb[:, k, :], ones[:, :], mh[:, k:k + 1], 1.0 / N,
                                                ALU.mult, ALU.mult).then_inc(mh_ready, 1)
                    dve.wait_ge(all_ready, 1)
                    if l == 2:
                        nc.vector.tensor_tensor(dsh[:, :, 0:2], sd[:, :, 1:3],
                                                allred[:, 0:2].unsqueeze(1).to_broadcast([P, T, 2]), ALU.subtract).then_inc(sub_ready, 1)
                        link(nc.vector.tensor_scalar(ssh[:, 0, :], sd[:, :, 0], allred[:, 0:1], 0.0, ALU.add, ALU.max))
                        link(nc.vector.tensor_scalar(ssh[:, 1, :], sd[:, :, 0], -1.0, allred[:, 1:2], ALU.mult, ALU.add))
                        nc.vector.tensor_scalar(ssh[:, 1, :], ssh[:, 1, :], 0.0, 100.0, ALU.max, ALU.min).then_inc(sub_ready, 1)
                    else:
                        nc.vector.tensor_tensor(dsh[:, :, :], sd[:, :, H:2 * H],
                                                allred[:, :].unsqueeze(1).to_broadcast([P, T, H]), ALU.subtract).then_inc(sub_ready, 1)
                        link(nc.vector.tensor_tensor(ssh[:, :, :], sd[:, :, 0:H].rearrange("p t h -> p h t"),
                                                     allred[:, :].unsqueeze(2).to_broadcast([P, H, T]), ALU.add))
                        nc.vector.tensor_scalar(ssh[:, :, :], ssh[:, :, :], 0.0, None, ALU.max).then_inc(sub_ready, 1)
                    dve.wait_ge(rt_done, 1)
                    nc.vector.tensor_copy(rT[0:NR, :], tp[0][0:NR, 0:P]).then_inc(rT_ready, 1)
                    if l != 2:
                        dve.wait_ge(exp_ready, 1)
                        nc.vector.tensor_tensor(bv[:, :, :], bco[:, :, :], vco[:, :, :], ALU.mult).then_inc(bv_ready, 1)
                        dve.wait_ge(bv_ready, 1)
                        nc.vector.tensor_scalar(vco[:, :, :], vco[:, :, :], ZSCALE, None, ALU.mult).then_inc(bv_ready, 1)
                        nc.vector.tensor_scalar(rr[:, :, :], rr[:, :, :], 1.0 / ZSCALE, None, ALU.mult)
                        nc.vector.tensor_copy(braw[:, :, :], bco[:, :, :])
                        nc.vector.tensor_scalar(bco[:, :, :], bco[:, :, :], BIG, None, ALU.mult)
                    dve.wait_ge(mean_done, 1)
                    if l == 2:
                        mb = meanbc[:, :, :].rearrange("p h e -> p (h e)")
                        nc.vector.memset(mb[:, D:E1], 1.0)
                        nc.vector.tensor_copy(mb[:, 0:D], fo[0][:, 0:D])
                    else:
                        nc.vector.memset(meanbc[:, :, O:EH], 1.0)
                        nc.vector.tensor_copy(meanbc[:, :, 0:O], fo[0][:, 0:D].rearrange("p (h o) -> p h o", h=H))
                        dve.sem_inc(zf_free, 2 * G)
                        with dve.Fori(0, T // G // 2) as pair:
                            for s in range(2):
                                t0 = pair * 2 + s
                                for p in range(G):
                                    t = t0 * G + p
                                    dve.wait_ge(first, t * 2 + 2)
                                    nc.vector.tensor_tensor(at(Zh, t)[:, :, (QB + 1) * EH:EZ], zf[:, s * G + p, :, :],
                                                            at(Zh, t)[:, :, QB * EH:(QB + 1) * EH], ALU.subtract)
                                    nc.vector.tensor_tensor(rest[:, s * G + p, :, :], bf[:, s * G + p, :, :], at(Z, t)[:, :, 0:EH],
                                                            ALU.subtract).then_inc(rest_ready, 1)
                                for p in range(G):
                                    t = t0 * G + p
                                    dve.wait_ge(second, t + 1)
                                    nc.vector.tensor_tensor(at(Z, t)[:, :, 2 * EH:3 * EH], rest[:, s * G + p, :, :], at(Z, t)[:, :, EH:2 * EH],
                                                            ALU.subtract).then_inc(zf_free, 1)

                @block.gpsimd
                def _(pool):
                    pool.wait_ge(red_ready, 1)
                    nc.gpsimd.partition_all_reduce(allred[:, 0:n], red[:, 0:n], P, RMAX).then_inc(all_ready, 1)
                    if l != 2:
                        pool.wait_ge(bv_ready, 2)
                        with pool.Fori(0, T // G // 2) as pair:
                            for s in range(2):
                                t0 = pair * 2 + s
                                for p in range(G):
                                    t = t0 * G + p
                                    pool.wait_ge(zf_free, t + 1)
                                    pool.sem_inc(bv_ready, 1)
                                    nc.gpsimd.tensor_tensor(zf[:, s * G + p, :, :], at(F, t), at(vco, t).unsqueeze(2).to_broadcast([P, H, EH]), ALU.mult)
                                    nc.gpsimd.tensor_tensor(bf[:, s * G + p, :, :], at(F, t), at(bv, t).unsqueeze(2).to_broadcast([P, H, EH]),
                                                            ALU.mult).then_inc(zf_ready, 1)

                @block.scalar
                def _(act):
                    act.wait_ge(sub_ready, 2)
                    if l == 2:
                        nc.scalar.activation(rr[:, 0:2, :], ssh[:, 0:2, :], ACT.Exp, scale=-0.8).then_inc(rr_ready, 1)
                        nc.scalar.activation(bco[:, :, 0:2], dsh[:, :, 0:2], ACT.Exp, scale=0.8)
                        nc.scalar.activation(vco[:, :, 0:2], dsh[:, :, 0:2], ACT.Exp, scale=0.2)
                    else:
                        nc.scalar.activation(rr[:, :, :], ssh[:, :, :], ACT.Exp, scale=-0.8).then_inc(rr_ready, 1)
                        nc.scalar.activation(bco[:, :, :], dsh[:, :, :], ACT.Exp, scale=0.8)
                        nc.scalar.activation(vco[:, :, :], dsh[:, :, :], ACT.Exp, scale=0.2).then_inc(exp_ready, 1)
                        with act.Fori(0, T // G // 2) as pair:
                            for s in range(2):
                                t0 = pair * 2 + s
                                for p in range(G):
                                    t = t0 * G + p
                                    act.wait_ge(zf_ready, t + 1)
                                    nc.scalar.activation(at(Zh, t)[:, :, QB * EH:(QB + 1) * EH], zf[:, s * G + p, :, :], ACT.Copy).then_inc(first, 1)
                                    nc.scalar.activation(at(Z, t)[:, :, 0:EH], bf[:, s * G + p, :, :], ACT.Copy).then_inc(first, 1)
                                for p in range(G):
                                    t = t0 * G + p
                                    act.wait_ge(rest_ready, t + 1)
                                    nc.scalar.activation(at(Z, t)[:, :, EH:2 * EH], rest[:, s * G + p, :, :], ACT.Copy).then_inc(second, 1)

                @block.tensor
                def _(pe):
                    pe.wait_ge(mh_ready, 2)
                    if l != 2:
                        pe.wait_ge(w_loaded, 16)
                    for k in range(2):
                        if l == 2:
                            last = nc.tensor.matmul(fo[0][:, k * P:(k + 1) * P], mhb[:, k, :], ident[:, :], start=True, stop=True)
                        else:
                            last = nc.tensor.matmul(fo[0][:, 0:D], mhb[:, k, :], wr[:, k, 0:D], start=(k == 0), stop=(k == 1))
                    last.then_inc(mean_done, 1)
                    pe.wait_ge(rr_ready, 1)
                    nc.tensor.transpose(tp[0][0:NR, 0:P], rr[:, :, :].rearrange("p h t -> p (h t)")[:, 0:NR], ident[:, :]).then_inc(rt_done, 1)

                @block.sync
                def _(sp):
                    if l != 2:
                        sp.dma_start(wr[:, :, :].rearrange("p k c -> p (k c)"), proj[0 if l == 0 else 1]).then_inc(w_loaded, 16)
                    sp.wait_ge(rT_ready, 1)
                    sp.dma_start(rows.rearrange("h (t p) -> (h t) p", p=P)[0:NR, :], rT[0:NR, :]).then_inc(rows_stored, 16)
                    sp.wait_ge(rows_stored, 16)

        def gat(l, Z):
            NS = T // 2
            R = 8
            CH = 2 * R
            NC = T // CH
            FUSED = (0, 2)
            rows_loaded = [sem(f"rows_loaded{l}_{s}") for s in range(2)]
            mask_loaded = [sem(f"mask_loaded{l}_{c}") for c in range(NC)]
            step_ready = sem(f"step_ready{l}")
            a_ready = sem(f"a_ready{l}")
            rest_ready = sem(f"a_rest_ready{l}")
            used = sem(f"used{l}")
            acc_ready = sem(f"acc_ready{l}")
            acc_free = sem(f"acc_free{l}")
            e_free = sem(f"e_free{l}")
            banks = [acc, [tp[0], tp[1], fo[0], fo[1]]]
            chain = sem(f"pool_chain{l}")
            sp_step = sem(f"sp_step{l}")
            flag_turn = sem(f"flag_turn{l}")
            with ExitStack() as scope, nc.Block() as block:
                sb = tensors(scope)
                mask = sb(f"mask{l}", [P, T, B], bf16)
                rbc = sb(f"rbc{l}", [P, 2, B], f32)
                cut = sb(f"cut{l}", [P, R, 2, 2, B], bf16)
                e = sb(f"e{l}", [P, TB, EZ], f32)
                su = sb(f"su{l}", [P, TB, EH], f32)
                sw = sb(f"sw{l}", [P, TB, EH], f32)
                fl = sb(f"fl{l}", [P, TB], f32)
                fm = sb(f"fm{l}", [P, TB, EH], f32)
                rc = sb(f"rc{l}", [P, TB], f32)
                Zh = Z[:, :, :, :].bitcast(fp16)
                maskd = maskT.rearrange("b p (t i) -> b p t i", t=T)

                @block.sync
                def _(sp):
                    def hold(s_, value):
                        sp.wait_ge(s_, value)
                        sp.sem_inc(sp_step, 1)

                    def load_rows(b, h):
                        sp.dma_start(rbc[:, h % 2, :], rows[h:h + 1, bass.ds(b * B, B)].squeeze(0).partition_broadcast(P)
                                     ).then_inc(rows_loaded[h % 2], 16)

                    load_rows(0, 0)
                    load_rows(0, 1)

                    def later_rows(b):
                        for h in range(2, H):
                            hold(step_ready, (b * H + h - 1) * NS)
                            load_rows(b, h)

                    with sp.Fori(0, NB - 1) as b:
                        later_rows(b)
                        hold(step_ready, (b * H + 3) * NS)
                        load_rows(b + 1, 0)
                        hold(step_ready, (b * H + 4) * NS)
                        load_rows(b + 1, 1)
                    later_rows(NB - 1)

                @block.scalar
                def _(act):
                    act.sem_inc(acc_free, TB)

                    def step(n, h, jp, slot, tiles=2):
                        act.wait_ge(used, n + 1)
                        for q in range(tiles):
                            last = nc.scalar.activation(cut[:, slot, 0, q, :], rbc[:, h % 2, :], ACT.Sigmoid,
                                                        bias=bco[:, bass.ds(jp * 2 + q, 1), h:h + 1].squeeze(1), scale=-BIG)
                        last.then_inc(step_ready, 1)

                    def take(u, bank):
                        act.wait_ge(acc_ready, u + 1)
                        act.wait_ge(e_free, u + 1)
                        for i in range(TB):
                            nc.scalar.activation(e[:, i, :], bank[i][:, 0:EZ], ACT.Copy).then_inc(acc_free, 1)

                    with act.Fori(0, NB) as b:
                        for h in range(H):
                            u = b * H + h
                            act.wait_ge(rows_loaded[h % 2], 16 * (b * 2 + h // 2 + 1))
                            for k in range(R):
                                step(u * NS + k, h, k, k, 1 if k in FUSED else 2)
                            take(u, banks[(h + 1) % 2])
                            with act.Fori(0, NS // R - 1) as it:
                                for k in range(R):
                                    step(u * NS + it * R + R + k, h, it * R + R + k, k)
                    take(NB * H, banks[1])

                @block.vector
                def _(dve):
                    def unit(b, h):
                        u = b * H + h

                        def run(n0, jp0, fused=()):
                            def m(k):
                                return mask[:, bass.ds((jp0 + k) * 2, 2), :]
                            for k in range(R + 1):
                                if k < R:
                                    dve.wait_ge(step_ready, n0 + k + 1)
                                    if k in fused:
                                        nc.vector.tensor_tensor(cut[:, k, 0, 0, :], cut[:, k, 0, 0, :], m(k)[:, 0, :], ALU.mult)
                                        nc.vector.scalar_tensor_tensor(
                                            out=cut[:, k, 0, 1, :], in0=rbc[:, h % 2, :], scalar=braw[:, (jp0 + k) * 2 + 1, h:h + 1],
                                            in1=m(k)[:, 1, :], op0=ALU.is_lt, op1=ALU.mult).then_inc(a_ready, 1)
                                    else:
                                        nc.vector.tensor_tensor(cut[:, k, 0, :, :], cut[:, k, 0, :, :], m(k), ALU.mult).then_inc(a_ready, 1)
                                if k > 0:
                                    dve.wait_ge(a_ready, n0 + k)
                                    nc.vector.tensor_tensor(cut[:, k - 1, 1, :, :], m(k - 1), cut[:, k - 1, 0, :, :],
                                                            ALU.subtract).then_inc(rest_ready, 1)

                        if h == 0:
                            for c in range(NC):
                                dve.wait_ge(mask_loaded[c], 16 * (b + 1))
                                run(u * NS + c * R, c * R, FUSED if c == 0 else ())
                        else:
                            run(u * NS, 0, FUSED)
                            with dve.Fori(0, NS // R - 1) as it:
                                run(u * NS + it * R + R, it * R + R)

                    for i in range(TB):
                        last = nc.vector.memset(banks[1][i][:, 0:EZ], 0.0)
                    last.then_inc(acc_ready, 1)
                    with dve.Fori(0, NB) as b:
                        for h in range(H):
                            unit(b, h)

                @block.tensor
                def _(pe):
                    pe.sem_inc(used, R)

                    def edge(i, start):
                        return nc.tensor.matmul(bank[i][:, 0:2], zerob[:, :], identb[:, 0:2], start=start, stop=not start,
                                                skip_group_check=True)

                    with pe.Fori(0, NB) as b:
                        for h in range(H):
                            u = b * H + h
                            bank = banks[h % 2]
                            for i in range(TB):
                                pe.wait_ge(acc_free, u * TB + i + 1)
                                edge(i, True)
                            with pe.Fori(0, NS // R) as it:
                                for k in range(R):
                                    n = u * NS + it * R + k
                                    for part in range(2):
                                        pe.wait_ge(rest_ready if part else a_ready, n + 1)
                                        z = Zh if part else Z
                                        c0, c1 = (QB * EH, EZ) if part else (0, QB * EH)
                                        for q in range(2):
                                            for i in range(TB):
                                                last = nc.tensor.matmul(
                                                    bank[i][:, c0:c1], cut[:, k, part, q, i * P:(i + 1) * P],
                                                    z[:, bass.ds((it * R + k) * 2 + q, 1), h, c0:c1].squeeze(1),
                                                    start=False, stop=False, skip_group_check=True)
                                    last.then_inc(used, 1)
                            for i in range(TB):
                                last = edge(i, False)
                            last.then_inc(acc_ready, 1)

                @block.gpsimd
                def _(pool):
                    pool.sem_inc(e_free, 2)
                    K = 12

                    def load_mask(b, c):
                        pool.dma_start(mask[:, c * CH:(c + 1) * CH, :], maskd[bass.ds(b, 1), :, c * CH:(c + 1) * CH, :].squeeze(0)
                                       ).then_inc(mask_loaded[c], 16)

                    def add_head(b, h):
                        u = b * H + h
                        link = linker(pool, chain)
                        base = u * K

                        def part(q):
                            return e[:, :, q * EH:(q + 1) * EH]

                        pool.wait_ge(acc_free, (u + 3) * TB)
                        link(nc.gpsimd.tensor_tensor(su[:, :, :], part(1), part(2), ALU.add), base)
                        link(nc.gpsimd.tensor_tensor(sw[:, :, :], part(3), part(4), ALU.add), base)
                        link(nc.gpsimd.tensor_tensor(su[:, :, :], su[:, :, :], part(0), ALU.add), base)
                        pool.sem_inc(e_free, 1)
                        link(nc.gpsimd.tensor_tensor(sw[:, :, :], sw[:, :, :],
                                                     rr[:, h, bass.ds(b * TB, TB)].unsqueeze(2).to_broadcast([P, TB, EH]), ALU.mult), base)
                        link(nc.gpsimd.tensor_tensor(su[:, :, :], su[:, :, :], sw[:, :, :], ALU.add), base)
                        pool.sem_inc(flag_turn, 1)
                        link(nc.gpsimd.tensor_scalar(fl[:, :], su[:, :, O], 0.0, None, ALU.is_equal), base)
                        link(nc.gpsimd.tensor_tensor(fm[:, :, :], meanbc[:, h, :].unsqueeze(1).to_broadcast([P, TB, EH]),
                                                     fl[:, :].unsqueeze(2).to_broadcast([P, TB, EH]), ALU.mult), base)
                        link(nc.gpsimd.tensor_tensor(su[:, :, :], su[:, :, :], fm[:, :, :], ALU.add), base)
                        link(nc.gpsimd.tensor_tensor(rc[:, :], su[:, :, O], mone[:, :], ALU.pow), base)
                        link(nc.gpsimd.tensor_tensor(su[:, :, 0:O], su[:, :, 0:O],
                                                     rc[:, :].unsqueeze(2).to_broadcast([P, TB, O]), ALU.mult), base)
                        xs = x_sb[:, bass.ds(b * TB, TB), h * O:(h + 1) * O]
                        link(nc.gpsimd.tensor_tensor(xs, xs, su[:, :, 0:O], ALU.add), base)
                        pool.sem_inc(chain, 1)

                    for c in range(NC):
                        load_mask(0, c)
                    with pool.Fori(0, NB - 1) as b:
                        for h in range(H):
                            if h == H - 1:
                                for c in range(NC):
                                    pool.wait_ge(rest_ready, (b * H + 3) * NS + (c + 1) * R)
                                    pool.sem_inc(flag_turn, 1)
                                    load_mask(b + 1, c)
                            add_head(b, h)
                    for h in range(H):
                        add_head(NB - 1, h)

        def weighted_features(F, e, Z1):
            red_ready = sem("red_ready1")
            all_ready = sem("all_ready1")
            sub_ready = sem("sub_ready1")
            exp_ready = sem("exp_ready1")
            w_ready = sem("w_ready1")
            hi_ready = sem("z_hi_ready")
            with ExitStack() as scope, nc.Block() as block:
                sb = tensors(scope)
                red = sb("red1", [P, 1], f32)
                allred = sb("allred1", [P, 1], f32)
                w = sb("w1", [P, T], f32)

                @block.vector
                def _(dve):
                    nc.vector.reduce_max(red[:, :], e[:, 0, :], AXX).then_inc(red_ready, 1)
                    dve.wait_ge(all_ready, 1)
                    nc.vector.tensor_scalar(w[:, :], e[:, 0, :], allred[:, :], None, ALU.subtract).then_inc(sub_ready, 1)
                    dve.wait_ge(exp_ready, 1)
                    nc.vector.scalar_tensor_tensor(out=w[:, :], in0=e[:, 1, :], scalar=0.0, in1=w[:, :],
                                                   op0=ALU.not_equal, op1=ALU.mult).then_inc(w_ready, 1)
                    nc.vector.memset(Z1[:, :, :, E1:E2].bitcast(f32), 0.0)
                    with dve.Fori(0, T // G) as t0:
                        for p in range(G):
                            t = t0 * G + p
                            dve.wait_ge(hi_ready, t + 1)
                            nc.vector.scalar_tensor_tensor(out=Z1[:, bass.ds(t, 1), 1, 0:E1].squeeze(1), in0=at(F, t),
                                                           scalar=w[:, bass.ds(t, 1)],
                                                           in1=Z1[:, bass.ds(t, 1), 0, 0:E1].squeeze(1).bitcast(f32),
                                                           op0=ALU.mult, op1=ALU.subtract)

                @block.gpsimd
                def _(pool):
                    pool.wait_ge(red_ready, 1)
                    nc.gpsimd.partition_all_reduce(allred[:, :], red[:, :], P, RMAX).then_inc(all_ready, 1)

                @block.scalar
                def _(act):
                    act.wait_ge(sub_ready, 1)
                    nc.scalar.activation(w[:, :], w[:, :], ACT.Exp).then_inc(exp_ready, 1)
                    act.wait_ge(w_ready, 1)
                    with act.Fori(0, T // G) as t0:
                        for p in range(G):
                            t = t0 * G + p
                            nc.scalar.activation(Z1[:, bass.ds(t, 1), 0, 0:E1].squeeze(1), at(F, t), ACT.Copy,
                                                 scale=w[:, bass.ds(t, 1)]).then_inc(hi_ready, 1)

        def mask_product(Z1):
            mask_loaded = [sem(f"mask_loaded1_{c}") for c in range(NC)]
            R = 4
            wide_ready = sem("wide_ready")
            wide_used = sem("wide_used")
            acc_ready = sem("acc_ready1")
            acc_free = sem("acc_free1")
            den_ready = sem("den_ready1")
            sp_step = sem("sp_step1")
            act_step = sem("act_step1")
            banks = [acc, [tp[0], tp[1], fo[0], fo[1]]]
            with ExitStack() as scope, nc.Block() as block:
                sb = tensors(scope)
                mask = sb("mask1", [P, T, B], u8)
                wide = sb("wide", [P, R, B], f32r)
                den = sb("den1", [P, 2, TB], f32)
                maskd = maskT.rearrange("b p (t i) -> b p t i", t=T)

                @block.sync
                def _(sp):
                    def load_mask(b, c):
                        sp.dma_start(mask[:, c * CH:(c + 1) * CH, :], maskd[bass.ds(b, 1), :, c * CH:(c + 1) * CH, :].squeeze(0)
                                     ).then_inc(mask_loaded[c], 16)
                    for c in range(NC):
                        load_mask(0, c)
                    with sp.Fori(0, NB - 1) as b:
                        for c in range(NC):
                            sp.wait_ge(wide_ready, b * T + (c + 1) * CH)
                            sp.sem_inc(sp_step, 1)
                            load_mask(b + 1, c)

                @block.scalar
                def _(act):
                    with act.Fori(0, NB) as b:
                        for c in range(NC):
                            act.wait_ge(mask_loaded[c], 16 * b + 16)
                            act.sem_inc(act_step, 1)
                            with act.Fori(0, CH // R) as it:
                                for k in range(R):
                                    t = it * R + c * CH + k
                                    act.wait_ge(wide_used, b * T + t + 1)
                                    nc.scalar.activation(wide[:, k, :], at(mask, t), ACT.Copy).then_inc(wide_ready, 1)

                @block.tensor
                def _(pe):
                    pe.sem_inc(wide_used, R)
                    with pe.Fori(0, NB // 2) as pair:
                        for s in range(2):
                            b = pair * 2 + s
                            pe.wait_ge(acc_free, b + 1)
                            for i in range(TB):
                                nc.tensor.matmul(banks[s][i][:, 0:2], zerob[:, :], identb[:, 0:2], start=True, stop=False,
                                                 skip_group_check=True)
                            with pe.Fori(0, T // R) as it:
                                for k in range(R):
                                    t = it * R + k
                                    pe.wait_ge(wide_ready, b * T + t + 1)
                                    for i in range(TB):
                                        for part in range(2):
                                            last = nc.tensor.matmul(
                                                banks[s][i][:, 0:E2], wide[:, k, i * P:(i + 1) * P],
                                                Z1[:, bass.ds(t, 1), part, :].squeeze(1),
                                                start=False, stop=False, skip_group_check=True)
                                    last.then_inc(wide_used, 1)
                            for i in range(TB):
                                last = nc.tensor.matmul(banks[s][i][:, 0:2], zerob[:, :], identb[:, 0:2], start=False, stop=True,
                                                        skip_group_check=True)
                            last.then_inc(acc_ready, 1)

                @block.vector
                def _(dve):
                    dve.sem_inc(acc_free, 2)
                    with dve.Fori(0, NB // 2) as pair:
                        for s in range(2):
                            b = pair * 2 + s
                            dve.wait_ge(acc_ready, b + 1)
                            for i in range(TB):
                                nc.vector.tensor_scalar(den[:, s, i:i + 1], banks[s][i][:, D:E1], 1e-37, None, ALU.max).then_inc(den_ready, 1)
                            dve.wait_ge(den_ready, b * (TB + 1) + TB)
                            nc.vector.reciprocal(den[:, s, :], den[:, s, :]).then_inc(den_ready, 1)
                            dve.wait_ge(den_ready, (b + 1) * (TB + 1))
                            for i in range(TB):
                                xs = x_sb[:, bass.ds(b * TB + i, 1), :].squeeze(1)
                                last = nc.vector.scalar_tensor_tensor(out=xs, in0=banks[s][i][:, 0:D], scalar=den[:, s, i:i + 1], in1=xs,
                                                                      op0=ALU.mult, op1=ALU.add)
                            last.then_inc(acc_free, 1)

        def layer1():
            with ExitStack() as scope:
                Z1 = tensors(scope)("Z1", [P, T, 2, E2], f32r)
                with ExitStack() as inner:
                    F = tensors(inner)("F1", [P, T, E1], f32)
                    e = tensors(inner)("e1", [P, 2, T], f32)

                    def load_w(sp, wr, b_, a_, loaded):
                        sp.dma_start(wr[:, :, :], W1.rearrange("(k p) o -> p k o", k=2)).then_inc(loaded, 16)
                        sp.dma_start(b_[:, :], b1.partition_broadcast(P)).then_inc(loaded, 16)
                        sp.dma_start(a_[:, :], a1.rearrange("e z -> (e z)").partition_broadcast(P)).then_inc(loaded, 16)
                    features(1, load_w, D, {"F": F, "e": e})
                    weighted_features(F, e, Z1)
                mask_product(Z1)

        def signed_attention(X):
            R = 4
            mask_loaded = [sem(f"mask_loaded2_{c}") for c in range(NC)]
            rows_loaded = [sem(f"rows_loaded2_{s}") for s in range(2)]
            wt_loaded = sem("wt_loaded")
            wt_ready = sem("wt_ready")
            g_ready = sem("g_ready")
            hi_ready = sem("hi_ready")
            lo_ready = sem("lo_ready")
            used = sem("used2")
            acc_ready = sem("acc_ready2")
            acc_free = sem("acc_free2")
            norm_ready = sem("normalised")
            chain = sem("pool_chain2")
            flag_turn = sem("flag_turn2")
            turned = sem("turned2")
            t_ready = sem("t_ready2")
            y_ready = sem("y_ready")
            pos_ready = sem("pos_ready")
            neg_ready = sem("neg_ready")
            elu_free = sem("elu_free")
            sp_step = sem("sp_step2")
            add_step = sem("add_step")
            with ExitStack() as scope, nc.Block() as block:
                sb = tensors(scope)
                mask = sb("mask2", [P, T, B], u8)
                rbc = sb("rbc2", [P, 2, B], f32)
                fac = sb("factor", [P, R, B], f32)
                Ghi = sb("Ghi", [P, R, B], f32r)
                Glo = sb("Glo", [P, R, B], f32r)
                e = sb("e2", [P, 2, TB, E1], f32)
                fl = sb("fl2", [P, TB], f32)
                fm = sb("fm2", [P, TB, E1], f32)
                rc = sb("rc2", [P, TB], f32)
                wt = sb("wt", [P, 4, D], f32)
                ident = sb("ident_2", [P, P], f32)
                eT = sb("eT", [P, 2, 4, P], f32)
                pos = sb("pos", [P, 2, D], f32)
                neg = sb("neg", [P, 2, D], f32)
                maskd = maskT.rearrange("b p (t i) -> b p t i", t=T)

                @block.sync
                def _(sp):
                    def hold(s_, value):
                        sp.wait_ge(s_, value)
                        sp.sem_inc(sp_step, 1)

                    def load_mask(b, c):
                        sp.dma_start(mask[:, c * CH:(c + 1) * CH, :], maskd[bass.ds(b, 1), :, c * CH:(c + 1) * CH, :].squeeze(0)
                                     ).then_inc(mask_loaded[c], 16)

                    def load_rows(b, s):
                        sp.dma_start(rbc[:, s, :], rows[s:s + 1, bass.ds(b * B, B)].squeeze(0).partition_broadcast(P)
                                     ).then_inc(rows_loaded[s], 16)

                    sp.dma_start(wt[:, :, :], wtrans.rearrange("(k p) o -> p k o", p=P)).then_inc(wt_loaded, 16)
                    load_rows(0, 0)
                    load_rows(0, 1)
                    for c in range(NC):
                        load_mask(0, c)
                    with sp.Fori(0, NB - 1) as b:
                        hold(g_ready, (b * 2 + 1) * T)
                        load_rows(b + 1, 0)
                        for c in range(NC):
                            hold(g_ready, (b * 2 + 1) * T + (c + 1) * CH)
                            load_mask(b + 1, c)
                        load_rows(b + 1, 1)
                    sp.wait_ge(wt_loaded, 16)

                @block.vector
                def _(dve):
                    nc.vector.tensor_copy(ident[:, :], identb[:, :]).then_inc(wt_ready, 1)
                    dve.wait_ge(wt_loaded, 16)
                    nc.vector.tensor_scalar(wt[:, 2:4, :], wt[:, 2:4, :], -1.0, None, ALU.mult).then_inc(wt_ready, 1)

                    dve.sem_inc(lo_ready, R)

                    def weights(n0, s, t0, k0):
                        for p in range(2):
                            n = n0 + p
                            t = t0 + p
                            dve.wait_ge(lo_ready, n + 1)
                            nc.vector.scalar_tensor_tensor(out=fac[:, k0 + p, :], in0=rbc[:, s, :], scalar=bco[:, bass.ds(t, 1), s:s + 1].squeeze(1),
                                                           in1=at(mask, t), op0=ALU.max if s == 0 else ALU.min,
                                                           op1=ALU.mult).then_inc(g_ready, 1)

                    def lows(n0, s, t0, k0):
                        for p in range(2):
                            n = n0 + p
                            t = t0 + p
                            dve.wait_ge(hi_ready, n + 1)
                            nc.vector.scalar_tensor_tensor(out=Glo[:, k0 + p, :], in0=fac[:, k0 + p, :], scalar=vco[:, bass.ds(t, 1), s:s + 1].squeeze(1),
                                                           in1=Ghi[:, k0 + p, :].bitcast(f32), op0=ALU.mult,
                                                           op1=ALU.subtract).then_inc(lo_ready, 1)

                    with dve.Fori(0, NB) as b:
                        for s in range(2):
                            u = b * 2 + s
                            dve.wait_ge(rows_loaded[s], 16 * b + 16)
                            if s == 0:
                                for c in range(NC):
                                    dve.wait_ge(mask_loaded[c], 16 * b + 16)
                                    for t in range(c * CH, (c + 1) * CH, 2):
                                        weights(u * T + t, s, t, t % R)
                                        if t:
                                            lows(u * T + t - 2, s, t - 2, (t - 2) % R)
                            else:
                                weights(u * T, s, 0, 0)
                                with dve.Fori(0, T // R - 1) as it:
                                    for k in range(2, R + 2, 2):
                                        t = it * R + k
                                        weights(u * T + t, s, t, k % R)
                                        lows(u * T + t - 2, s, t - 2, k - 2)
                                weights(u * T + T - 2, s, T - 2, R - 2)
                                lows(u * T + T - 4, s, T - 4, R - 4)
                            lows(u * T + T - 2, s, T - 2, R - 2)

                @block.scalar
                def _(act):
                    act.sem_inc(acc_free, TB)

                    def highs(u, s, t0, count):
                        with act.Fori(0, count // R) as it:
                            for k in range(R):
                                t = it * R + t0 + k
                                act.wait_ge(used, u * T + t + 1)
                                act.wait_ge(g_ready, u * T + t + 1)
                                nc.scalar.activation(Ghi[:, k, :], fac[:, k, :], ACT.Copy,
                                                     scale=vco[:, bass.ds(t, 1), s:s + 1].squeeze(1)).then_inc(hi_ready, 1)

                    def take(u, s):
                        act.wait_ge(acc_ready, u + 1)
                        for i in range(TB):
                            nc.scalar.activation(e[:, s, i, :], acc[i][:, 0:E1], ACT.Copy).then_inc(acc_free, 1)

                    def elu(b):
                        for i in range(TB + 1):
                            if i < TB:
                                act.wait_ge(turned, b * TB + i + 1)
                                nc.scalar.activation(eT[:, i % 2, :, :].rearrange("p k c -> p (k c)"), tp[i % 2][:, :],
                                                     ACT.Copy).then_inc(t_ready, 1)
                            if i > 0:
                                n = b * TB + i - 1
                                p = (i - 1) % 2
                                act.wait_ge(y_ready, n + 1)
                                act.wait_ge(elu_free, n + 1)
                                nc.scalar.activation(pos[:, p, :], fo[p][:, 0:D], ACT.Relu).then_inc(pos_ready, 1)
                                nc.scalar.activation(neg[:, p, :], fo[p][:, 0:D], ACT.Relu, scale=-1.0).then_inc(pos_ready, 1)
                                act.wait_ge(pos_ready, 2 * n + 2)
                                nc.scalar.activation(neg[:, p, :], neg[:, p, :], ACT.Exp, scale=-1.0).then_inc(neg_ready, 1)

                    highs(0, 0, 0, T)
                    highs(1, 1, 0, R)
                    take(0, 0)
                    highs(1, 1, R, T - R)
                    with act.Fori(0, NB - 1) as b:
                        u = b * 2 + 2
                        highs(u, 0, 0, R)
                        take(u - 1, 1)
                        highs(u, 0, R, T // 2 - R)
                        elu(b)
                        highs(u, 0, T // 2, T // 2)
                        highs(u + 1, 1, 0, R)
                        take(u, 0)
                        highs(u + 1, 1, R, T - R)
                    take(2 * NB - 1, 1)
                    elu(NB - 1)

                @block.tensor
                def _(pe):
                    pe.sem_inc(used, R)
                    pe.wait_ge(wt_ready, 2)

                    def edge(i, start):
                        return nc.tensor.matmul(acc[i][:, 0:2], zerob[:, :], identb[:, 0:2], start=start, stop=not start,
                                                skip_group_check=True)

                    def opened(u):
                        for i in range(TB):
                            pe.wait_ge(acc_free, u * TB + i + 1)
                            edge(i, True)

                    def products(u, t0, count):
                        with pe.Fori(0, count // R) as it:
                            for k in range(R):
                                t = it * R + t0 + k
                                for w, q in ((Ghi, 0), (Ghi, 1), (Glo, 0)):
                                    if w is Glo:
                                        pe.wait_ge(lo_ready, u * T + t + 1 + R)
                                    elif q == 0:
                                        pe.wait_ge(hi_ready, u * T + t + 1)
                                    for i in range(TB):
                                        last = nc.tensor.matmul(acc[i][:, 0:E2], w[:, k, i * P:(i + 1) * P],
                                                                X[:, bass.ds(t, 1), q, :].squeeze(1),
                                                                start=False, stop=False, skip_group_check=True)
                                last.then_inc(used, 1)

                    def closed():
                        for i in range(TB):
                            last = edge(i, False)
                        last.then_inc(acc_ready, 1)

                    def project(b):
                        pe.wait_ge(norm_ready, 2 * b + 2)
                        for i in range(TB + 1):
                            if i < TB:
                                for s in range(2):
                                    for k in range(2):
                                        last = nc.tensor.transpose(tp[i % 2][:, (s * 2 + k) * P:(s * 2 + k + 1) * P],
                                                                   e[:, s, i, k * P:(k + 1) * P], ident[:, :])
                                last.then_inc(turned, 1)
                            if i > 0:
                                pe.wait_ge(t_ready, b * TB + i)
                                p = (i - 1) % 2
                                for k in range(4):
                                    last = nc.tensor.matmul(fo[p][:, 0:D], eT[:, p, k, :], wt[:, k, :], start=(k == 0), stop=(k == 3))
                                last.then_inc(y_ready, 1)

                    def unit(u):
                        opened(u)
                        products(u, 0, T)
                        closed()

                    unit(0)
                    unit(1)
                    with pe.Fori(0, NB - 1) as b:
                        u = b * 2 + 2
                        opened(u)
                        products(u, 0, T // 2)
                        project(b)
                        products(u, T // 2, T // 2)
                        closed()
                        unit(u + 1)
                    project(NB - 1)

                @block.gpsimd
                def _(pool):
                    pool.sem_inc(elu_free, 2)
                    K = 5

                    def normalise(u, s):
                        link = linker(pool, chain)
                        es = e[:, s, :, :]
                        pool.wait_ge(acc_free, (u + 1) * TB + TB)
                        pool.sem_inc(flag_turn, 1)
                        link(nc.gpsimd.tensor_scalar(fl[:, :], es[:, :, D], 0.0, None, ALU.is_equal), u * K)
                        link(nc.gpsimd.tensor_tensor(fm[:, :, :], meanbc[:, :, :].rearrange("p h e -> p (h e)")[:, 0:E1].unsqueeze(1)
                                                     .to_broadcast([P, TB, E1]),
                                                     fl[:, :].unsqueeze(2).to_broadcast([P, TB, E1]), ALU.mult), u * K)
                        link(nc.gpsimd.tensor_tensor(es, es, fm[:, :, :], ALU.add), u * K)
                        link(nc.gpsimd.tensor_tensor(rc[:, :], es[:, :, D], mone[:, :], ALU.pow), u * K)
                        nc.gpsimd.tensor_tensor(es[:, :, 0:D], es[:, :, 0:D], rc[:, :].unsqueeze(2).to_broadcast([P, TB, D]),
                                                ALU.mult).then_inc(norm_ready, 1)
                        pool.wait_ge(norm_ready, u + 1)
                        pool.sem_inc(chain, 1)

                    def add(b):
                        for i in range(TB):
                            n = b * TB + i
                            pool.wait_ge(neg_ready, n + 1)
                            nc.gpsimd.tensor_tensor(neg[:, i % 2, :], neg[:, i % 2, :], mone[:, 0:1].to_broadcast([P, D]), ALU.add).then_inc(add_step, 1)
                            pool.wait_ge(add_step, 3 * n + 1)
                            nc.gpsimd.tensor_tensor(pos[:, i % 2, :], pos[:, i % 2, :], neg[:, i % 2, :], ALU.add).then_inc(add_step, 1)
                            pool.wait_ge(add_step, 3 * n + 2)
                            xs = x_sb[:, bass.ds(n, 1), :].squeeze(1)
                            nc.gpsimd.tensor_tensor(xs, xs, pos[:, i % 2, :], ALU.add).then_inc(add_step, 1)
                            pool.wait_ge(add_step, 3 * n + 3)
                            pool.sem_inc(elu_free, 1)

                    normalise(0, 0)
                    normalise(1, 1)
                    with pool.Fori(0, NB - 1) as b:
                        add(b)
                        normalise(b * 2 + 2, 0)
                        normalise(b * 2 + 3, 1)
                    add(NB - 1)

        def layer2():
            with ExitStack() as scope:
                X = tensors(scope)("X2", [P, T, 2, E2], f32r)
                features(2, None, 2, {"X": X})
                factors(2)
                signed_attention(X)

        def store_x():
            stored = sem("stored")
            with nc.Block() as block:
                @block.sync
                def _(sp):
                    sp.dma_start(out.rearrange("(t p) d -> p t d", p=P), x_sb[:, :, :]).then_inc(stored, 16)
                    sp.wait_ge(stored, 16)

        def gat_layer(l, bias):
            with ExitStack() as scope:
                Z = tensors(scope)(f"Z{l}", [P, T, H, EZ], bf16)
                with ExitStack() as inner:
                    F = tensors(inner)(f"F{l}", [P, T, H, EH], f32)

                    def load_w(sp, wr, b_, _, loaded):
                        sp.dma_start(wr[:, :, :].rearrange("p k c -> p (k c)"), proj[0 if l == 0 else 1]).then_inc(loaded, 16)
                        if bias is not None:
                            sp.dma_start(b_[:, :], bias.rearrange("h o -> (h o)").partition_broadcast(P)).then_inc(loaded, 16)
                    stage = Z[:, :, :, :].rearrange("p t h e -> p (t h e)")[:, 0:T * B].bitcast(u8).rearrange("p (s t i) -> p s t i", s=2, t=T)
                    features(l, load_w, SC, {"F": F}, stage if l == 0 else None)
                    factors(l, F, Z)
                gat(l, Z)

        setup()
        gat_layer(0, b0)
        clear_semaphores()
        layer1()
        clear_semaphores()
        layer2()
        clear_semaphores()
        gat_layer(3, None)
        store_x()


_INS = ["x", "adj", "L0_gnn_W", "L0_gnn_a", "L0_gnn_b", "L1_gnn_W", "L1_gnn_b", "L1_gnn_a",
        "L2_gnn_W", "L2_gnn_a", "L2_gnn_wtrans", "L3_gnn_W", "L3_gnn_a"]


def kernel(**inputs):
    import numpy as _np
    import concourse.bacc as _bacc
    from concourse import mybir as _mybir
    from concourse.bass_utils import run_bass_kernel_spmd as _run

    nc = _bacc.Bacc("TRN2", target_bir_lowering=False, num_devices=1)
    arrays, args = {}, []
    for name in _INS:
        a = _np.ascontiguousarray(inputs[name])
        arrays[f"in_{name}"] = a
        args.append(nc.dram_tensor(f"in_{name}", a.shape, _mybir.dt.from_np(a.dtype), kind="ExternalInput").ap())
    args.append(nc.dram_tensor("out_x", (N, D), f32, kind="ExternalOutput").ap())
    program(nc, *args)
    r = _run(nc, [arrays], core_ids=[0])
    return r.results[0]["out_x"]
```
